# Optimizing a Trainium2 kernel written in Bass

```python
import numpy as np
import jax
import jax.numpy as jnp

def _softmax(x, axis=-1):
    return jax.nn.softmax(x, axis=axis)

def _gelu(x):
    return jax.nn.gelu(x, approximate=True)

def _silu(x):
    return jax.nn.silu(x)

def _sigmoid(x):
    return jax.nn.sigmoid(x)

def _layernorm(x, axis=-1, eps=1e-05):
    m = jnp.mean(x, axis=axis, keepdims=True)
    v = jnp.var(x, axis=axis, keepdims=True)
    return (x - m) / jnp.sqrt(v + eps)

def _scatter_add(tgt, idx, src, axis=0):
    return tgt.at[idx].add(src)

def _segment_sum(src, seg, n):
    return jax.ops.segment_sum(src, seg, n)
kernel_name = 'mk_adaln_d1_jaxref_r8_c681f4'

def setup_inputs(seed: int=0):
    np.random.seed(seed)
    _w = jnp.asarray

    def _L0_attn_setup():
        import jax, jax.numpy as jnp
        import numpy as np
        NUM_HEADS = 16

        def _stablemax3_s(x):
            pos = 1.0 + x * (1.0 + 0.5 * x * (1.0 + x / 3.0))
            neg = 1.0 / (1.0 - x * (1.0 - 0.5 * x * (1.0 - x / 3.0)))
            return jnp.where(x >= 0, pos, neg)

        def stablemax3(logits, axis=-1):
            logits = logits - jnp.max(logits, axis=axis, keepdims=True)
            s = _stablemax3_s(logits)
            return s / jnp.sum(s, axis=axis, keepdims=True)
        key = jax.random.key(seed)
        k1, k2, k3 = jax.random.split(key, 3)
        B, S, D = (2, 256, 128)
        x = jax.random.normal(k1, (B, S, D), dtype=jnp.float32)
        w_qkv = jax.random.normal(k2, (3 * D, D), dtype=jnp.float32) * 0.02
        w_out = jax.random.normal(k3, (D, D), dtype=jnp.float32) * 0.02
        b_out = jnp.zeros((D,), dtype=jnp.float32)
        return {'x': x, 'w_qkv': w_qkv, 'w_out': w_out, 'b_out': b_out}
    _L0_attn_in = _L0_attn_setup()

    def _L0_ffn_setup():
        import jax, jax.numpy as jnp
        import numpy as np
        import math
        D_IN = 128
        FEATURES = (512, 512, 128)
        BATCH, SEQ = (8, 256)

        def _conn_dense(kernel_bool, x):
            w = jnp.where(kernel_bool, jnp.float32(1.0), jnp.float32(-1.0))
            return x @ w
        key = jax.random.key(seed)
        kx, kk0, kk1, kk2 = jax.random.split(key, 4)
        x = jax.random.normal(kx, (BATCH, SEQ, D_IN), dtype=jnp.float32)
        k0 = jax.random.randint(kk0, (2 * D_IN, FEATURES[0]), 0, 2).astype(jnp.bool_)
        k1 = jax.random.randint(kk1, (FEATURES[0], FEATURES[1]), 0, 2).astype(jnp.bool_)
        k2 = jax.random.randint(kk2, (FEATURES[1], FEATURES[2]), 0, 2).astype(jnp.bool_)
        s0 = jnp.asarray(1.0 / math.sqrt(2 * D_IN), dtype=jnp.float32)
        s1 = jnp.asarray(1.0 / math.sqrt(FEATURES[0]), dtype=jnp.float32)
        s2 = jnp.asarray(1.0 / math.sqrt(FEATURES[1]), dtype=jnp.float32)
        return {'x': x, 'k0': k0, 'k1': k1, 'k2': k2, 's0': s0, 's1': s1, 's2': s2}
    _L0_ffn_in = _L0_ffn_setup()
    _L0_c = _w((lambda *s: np.random.randn(*s).astype(np.float32) * 0.05)(8, 128))
    _L0_wmod = _w((lambda *s: np.random.randn(*s).astype(np.float32) * 0.05)(128, 6 * 128) * 128 ** (-0.5))
    _d = {'L0_attn_x': _L0_attn_in['x'], 'L0_attn_w_qkv': _L0_attn_in['w_qkv'], 'L0_attn_w_out': _L0_attn_in['w_out'], 'L0_attn_b_out': _L0_attn_in['b_out'], 'L0_ffn_k0': _L0_ffn_in['k0'], 'L0_ffn_k1': _L0_ffn_in['k1'], 'L0_ffn_k2': _L0_ffn_in['k2'], 'L0_ffn_s0': _L0_ffn_in['s0'], 'L0_ffn_s1': _L0_ffn_in['s1'], 'L0_ffn_s2': _L0_ffn_in['s2'], 'L0_c': _L0_c, 'L0_wmod': _L0_wmod}
    _x0 = _d['L0_attn_x']
    _d['L0_attn_x'] = jax.random.normal(jax.random.fold_in(jax.random.key(seed), 1), (8, 512, 128), dtype=_x0.dtype)
    del _x0
    return _d

def reference(L0_attn_x, L0_attn_w_qkv, L0_attn_w_out, L0_attn_b_out, L0_ffn_k0, L0_ffn_k1, L0_ffn_k2, L0_ffn_s0, L0_ffn_s1, L0_ffn_s2, L0_c, L0_wmod):

    def _L0_attn_ref(x, w_qkv, w_out, b_out):
        import jax, jax.numpy as jnp
        import numpy as np
        NUM_HEADS = 16

        def _stablemax3_s(x):
            pos = 1.0 + x * (1.0 + 0.5 * x * (1.0 + x / 3.0))
            neg = 1.0 / (1.0 - x * (1.0 - 0.5 * x * (1.0 - x / 3.0)))
            return jnp.where(x >= 0, pos, neg)

        def stablemax3(logits, axis=-1):
            logits = logits - jnp.max(logits, axis=axis, keepdims=True)
            s = _stablemax3_s(logits)
            return s / jnp.sum(s, axis=axis, keepdims=True)
        B, S, D = x.shape
        H = NUM_HEADS
        hd = D // H
        scale = hd ** (-0.5)
        qkv = x @ w_qkv.T
        qkv = qkv.reshape(B, S, 3, H, hd)
        qkv = jnp.transpose(qkv, (2, 0, 3, 1, 4))
        q, k, v = (qkv[0], qkv[1], qkv[2])
        attn = jnp.einsum('bhsd,bhtd->bhst', q, k) * scale
        attn = stablemax3(attn, axis=-1)
        out = jnp.einsum('bhst,bhtd->bhsd', attn, v)
        out = jnp.transpose(out, (0, 2, 1, 3)).reshape(B, S, D)
        return out @ w_out.T + b_out

    def _L0_ffn_ref(x, k0, k1, k2, s0, s1, s2):
        import jax, jax.numpy as jnp
        import numpy as np
        import math
        D_IN = 128
        FEATURES = (512, 512, 128)
        BATCH, SEQ = (8, 256)

        def _conn_dense(kernel_bool, x):
            w = jnp.where(kernel_bool, jnp.float32(1.0), jnp.float32(-1.0))
            return x @ w
        h = jnp.concatenate([x, -x], axis=-1)
        h = s0 * _conn_dense(k0, h)
        h = jax.nn.relu(h) * 2
        h = s1 * _conn_dense(k1, h)
        h = jax.nn.relu(h) * 2
        h = s2 * _conn_dense(k2, h)
        return h
    x = L0_attn_x
    mod = (_silu(L0_c) @ L0_wmod).reshape(L0_c.shape[0], 6, 1, -1)
    sa, ca, ga, sb, cb, gb = (mod[:, 0], mod[:, 1], mod[:, 2], mod[:, 3], mod[:, 4], mod[:, 5])
    ga = (2 * (ga >= 0) - 1) * jnp.maximum(jnp.abs(ga), 0.25)
    gb = (2 * (gb >= 0) - 1) * jnp.maximum(jnp.abs(gb), 0.25)
    h = _layernorm(x, axis=-1) * (1 + ca) + sa
    x = x + ga * _L0_attn_ref(h, L0_attn_w_qkv, L0_attn_w_out, L0_attn_b_out)
    h = _layernorm(x, axis=-1) * (1 + cb) + sb
    x = x + gb * _L0_ffn_ref(h, L0_ffn_k0, L0_ffn_k1, L0_ffn_k2, L0_ffn_s0, L0_ffn_s1, L0_ffn_s2)
    return x

_drawn_inputs = setup_inputs


def setup_inputs(seed=0):
    import zlib

    import numpy as np

    out = dict(_drawn_inputs(seed))
    spreads = {'L0_attn_b_out': (0.0, 0.341)}
    factors = {'L0_attn_w_qkv': 8.0, 'L0_attn_w_out': 8.0}
    for name, (base, spread) in spreads.items():
        noise = np.random.default_rng([zlib.crc32(name.encode()), seed]).standard_normal(out[name].shape)
        drawn = base * np.exp(spread * noise) if base else spread * noise
        out[name] = jnp.asarray(drawn.astype(out[name].dtype))
    for name, factor in factors.items():
        out[name] = (out[name] * factor).astype(out[name].dtype)
    return out
```

```python
from contextlib import ExitStack

import concourse.bass as bass
from concourse import mybir

F32 = mybir.dt.float32
BF16 = mybir.dt.bfloat16
U8 = mybir.dt.uint8
ALU = mybir.AluOpType
ACT = mybir.ActivationFunctionType
AX_X = mybir.AxisListType.X

P = 128
B = 8
S = 512
D = 128
H = 16
HD = D // H
QUAD = 4
NQ = H // QUAD
TB = S // P
HALF = 2 * S
F = 512
KC = F // P
PARTS = 3
NROW = PARTS * PARTS * HD
MROW = 96
EPS = 1e-5
LOADS = 11
SCALE = HD ** -0.5


PATHS = [("D", "D") for n in range(H)]
P_RING = 8
F_RING = 2

LAG = 2


def before(kinds, n, h):
    return sum(PATHS[m][k] in kinds for m in range(H) for k in range(2) if (m, k) <= (n, h))


N_D = before("D", H, 0)
N_A = before("A", H, 0)
N_V = before("V", H, 0)
N_P = N_A + N_V
assert N_D % 2 == 0 and N_P % 2 == 0

MISC = [
    (0, 0, "hT", 1), (0, 1, "mT0", 0), (1, 0, "q", 1), (2, 0, "k", 1), (3, 0, "h2T", -2), (3, 1, "l0_0", -2),
    (4, 0, "l0_1", -2), (4, 1, "mT1", 0), (5, 0, "l0_2", -2), (5, 1, "l0_3", -2), (6, 0, "l1_0", -2),
    (7, 0, "l1_1", -2), (8, 1, "mT2", 0), (9, 0, "l1_2", -2), (10, 0, "proj", -1), (10, 1, "x1", -1),
    (11, 0, "l1_3", -2), (12, 0, "v", 1), (12, 1, "mT3", 1), (13, 0, "l2", -2), (14, 0, "y", -2),
]
LONG = ("l1_0", "l1_1", "l1_2", "l1_3", "l2")


def live(beta):
    return not isinstance(beta, int) or 0 <= beta < B


def adaln_block(nc, x, w_qkv, w_out, b_out, k0, k1, k2, s0, s1, s2, c, wmod, out):
    x_t = x.rearrange("b (t p) d -> p (b t) d", p=P)
    out_t = out.rearrange("b (t p) d -> p (b t) d", p=P)

    with ExitStack() as ctx:
        def sb(name, shape, dt=F32):
            return ctx.enter_context(nc.sbuf_tensor(name, shape, dt))

        def sem(name):
            return ctx.enter_context(nc.semaphore(name))

        Z = ctx.enter_context(nc.psum_tensor("Z", [P, 2, HALF], F32))
        SA = ctx.enter_context(nc.psum_tensor("SA", [P, 2, S], F32))
        OP = ctx.enter_context(nc.psum_tensor("OP", [P, S], F32))
        MB = ctx.enter_context(nc.psum_tensor("MB", [P, S], F32))
        MB4 = MB[:, :].rearrange("p (t d) -> p t d", t=TB)

        QH = sb("QH", [P, H, S], BF16)
        KH = sb("KH", [P, H, S], BF16)
        prob = sb("prob", [P, P_RING, TB * S])
        cub = sb("cub", [P, F_RING, 2, HALF])
        sq = sb("sq", [P, 2, HALF])
        zc = sb("zc", [P, 2, HALF])
        Vq = sb("Vq", [P, TB, H, 2 * HD])
        Vn = sb("Vn", [P, TB, H, HD])
        SQ = sb("SQ", [P, PARTS, S], BF16)
        SK = sb("SK", [P, PARTS, S], BF16)
        rem = sb("rem", [P, 2, S])
        mx = sb("mx", [P, 2, QUAD * TB])
        ms = sb("ms", [QUAD * TB, P])
        mrem = sb("mrem", [QUAD * TB, P])
        mp = sb("mp", [QUAD * TB, PARTS, P], BF16)
        OT = sb("OT", [P, 2, S])
        num = sb("num", [P, S])
        den = sb("den", [P, S])
        xa = sb("xa", [P, TB, D])
        xn = sb("xn", [P, TB, D])
        hT = sb("hT", [P, S])
        xb = sb("xb", [P, TB, D])
        z12 = sb("z12", [P, S])
        x1 = sb("x1", [P, TB, D])
        x1k = sb("x1k", [P, TB, D])
        x1n = sb("x1n", [P, TB, D])
        h2T = sb("h2T", [P, S])
        hid = [sb("hid0", [P, KC, S]), sb("hid1", [P, KC, S])]
        y = sb("y", [P, TB, D])
        wq = sb("wq", [P, D])
        wk = sb("wk", [P, D])
        wv = sb("wv", [P, D])
        wo = sb("wo", [P, D])
        W0 = sb("W0", [P, F])
        W1 = sb("W1", [P, KC, F])
        W2 = sb("W2", [P, KC, D])
        ident = sb("ident", [P, P])
        mod = sb("mod", [P, 8, B])
        gtmp = sb("gtmp", [P, 3, B])
        sv = sb("sv", [P, 3])
        bo = sb("bo", [P, 1])
        st1 = sb("st1", [P, TB, 6])
        mv1 = sb("mv1", [P, TB, 2])
        rs1 = sb("rs1", [P, TB])
        st2 = sb("st2", [P, TB, 6])
        mv2 = sb("mv2", [P, TB, 2])
        rs2 = sb("rs2", [P, TB])
        epst = sb("epst", [P, 1])

        stage = prob[:, 0, :]
        w_rows = stage[:, 0:4 * D].rearrange("p (k d) -> p k d", k=4)
        wm = stage[:, 512:512 + 6 * D]
        cT = stage[:, 1280:1280 + B]
        csil = stage[:, 1296:1296 + B]
        c_rows = stage[0:B, 1408:1408 + D]
        c_exp = stage[0:B, 1536:1536 + D]
        c_inv = stage[0:B, 1664:1664 + D]
        c_sil = stage[0:B, 1792:1792 + D]
        k_u8 = prob[:, 1, :].bitcast(U8)
        k0u = k_u8[:, 0:2 * F].rearrange("p (a n) -> p a n", a=2)
        k1u = k_u8[:, 1024:1024 + KC * F].rearrange("p (a n) -> p a n", a=KC)
        k2u = k_u8[:, 4096:4096 + KC * D].rearrange("p (a n) -> p a n", a=KC)

        s_ld = sem("s_ld")
        s_id = sem("s_id")
        s_apart = sem("s_apart")
        s_su_pe = sem("s_su_pe")
        s_su_v = sem("s_su_v")
        s_su_a = sem("s_su_a")
        s_su_g = sem("s_su_g")
        s_z = sem("s_z")
        s_sq = sem("s_sq")
        s_za = sem("s_za")
        s_zv = sem("s_zv")
        s_cv = sem("s_cv")
        s_q1 = sem("s_q1")
        s_cp = sem("s_cp")
        s_ln = sem("s_ln")
        s_p = sem("s_p")
        s_pv = sem("s_pv")
        s_a = sem("s_a")
        s_mx = sem("s_mx")
        s_ms = sem("s_ms")
        s_mp = sem("s_mp")
        s_mrow = [sem(f"s_mrow{g}") for g in range(NQ)]
        s_qk = [sem(f"s_qk{g}") for g in range(NQ)]
        s_ot = sem("s_ot")
        s_gat = [sem(f"s_gat{g}") for g in range(2)]
        s_vq = sem("s_vq")
        s_one = sem("s_one")
        s_ones_k = sem("s_ones_k")
        s_made = {m[2]: sem("made_" + m[2]) for m in MISC}
        s_taken = {m[2]: sem("taken_" + m[2]) for m in MISC}
        s_part1 = sem("s_part1")
        s_part2 = sem("s_part2")
        s_part3 = sem("s_part3")
        s_xa = sem("s_xa")
        s_xb = sem("s_xb")
        s_st1 = sem("s_st1")
        s_mv1 = sem("s_mv1")
        s_ln1 = sem("s_ln1")
        s_rs1 = sem("s_rs1")
        s_xn = sem("s_xn")
        s_st2 = sem("s_st2")
        s_mv2 = sem("s_mv2")
        s_ln2 = sem("s_ln2")
        s_rs2 = sem("s_rs2")
        s_x1n = sem("s_x1n")
        s_x1k = sem("s_x1k")
        s_dln = sem("s_dln")
        s_dinv = sem("s_dinv")
        s_att = sem("s_att")
        s_out = sem("s_out")

        def need(eng, s, n):
            if not isinstance(n, int) or n > 0:
                eng.wait_ge(s, n)

        def apart(eng, b):
            if not isinstance(b, int):
                eng.sem_inc(s_apart)

        def z_taken(eng, b, n, h):
            kind = PATHS[n][h]
            s, per = {"D": (s_cv, N_D), "A": (s_za, N_A), "V": (s_zv, N_V)}[kind]
            need(eng, s, b * per + before(kind, n, h))

        def cubic_ready(eng, b, n, h):
            if PATHS[n][h] == "D":
                need(eng, s_cv, b * N_D + before("D", n, h))
            else:
                need(eng, s_cp, b * N_P + before("AV", n, h))

        def batches(body):
            def run(eng):
                for b in range(-2, 3):
                    body(b)
                with eng.Fori(3, B - 2) as b:
                    body(b)
                for b in range(B - 2, B + 2):
                    body(b)
            return run

        def col(i, b):
            return mod[:, i, bass.ds(b, 1)]

        block = ctx.enter_context(nc.Block())

        def pe_setup(pe):
            pe.wait_ge(s_id, 2)
            pe.wait_ge(s_ld, LOADS * 16)
            for i in range(4):
                mm = nc.tensor.transpose(MB4[:, i, :], w_rows[:, i, :], ident[:, :])
            mm.then_inc(s_su_pe, 1)
            pe.wait_ge(s_su_v, 9)
            nc.tensor.transpose(MB[:, 0:B], c_sil, ident[0:B, 0:B]).then_inc(s_su_pe, 1)
            pe.wait_ge(s_su_v, 10)
            for i in range(6):
                mm = nc.tensor.matmul(MB[:, 64 + i * B:64 + (i + 1) * B], wm[:, i * D:(i + 1) * D], csil,
                                      start=True, stop=True)
            mm.then_inc(s_su_pe, 1)
            pe.wait_ge(s_su_v, 19)
            pe.wait_ge(s_one, 3)
            pe.wait_ge(s_ones_k, 1)

        def misc_prev(b, i):
            while True:
                i, b = (i - 1, b) if i else (len(MISC) - 1, b - 1)
                if live(b + MISC[i][3]):
                    return MISC[i][2], b + MISC[i][3]
                if isinstance(b, int) and b < -2:
                    return None

        def misc_product(pe, b, i, second=False):
            _, _, name, off = MISC[i]
            beta = b + off
            if not live(beta):
                return
            prev = misc_prev(b, i)
            if prev and not second:
                need(pe, s_taken[prev[0]], prev[1] + 1)
            if name == "hT":
                pe.wait_ge(s_xn, beta + 1)
                for t in range(TB):
                    mm = nc.tensor.transpose(MB4[:, t, :], xn[:, t, :], ident[:, :])
            elif name[:2] == "mT":
                g = int(name[2])
                need(pe, s_mx, 64 * beta + 16 * ((g + 1) % NQ if name != "mT3" else 0) + 16)
                gg = (g + 1) % NQ
                mm = nc.tensor.transpose(MB[0:QUAD * TB, 0:P], mx[:, gg % 2, :], ident[:, :])
            elif name in "qk":
                pe.wait_ge(s_taken["hT"], beta + 1)
                mm = nc.tensor.matmul(MB[:, :], (wq if name == "q" else wk)[:, :], hT[:, :], start=True, stop=True)
            elif name == "v":
                for t in range(TB):
                    mm = nc.tensor.matmul(MB4[:, t, :], hT[:, t * P:(t + 1) * P], wv[:, :], start=True, stop=True)
            elif name == "proj":
                pe.wait_ge(s_att, beta + 1)
                mm = nc.tensor.matmul(MB[:, :], wo[:, :], num[:, :], start=True, stop=True)
            elif name == "x1":
                pe.wait_ge(s_taken["proj"], beta + 1)
                for t in range(TB):
                    mm = nc.tensor.transpose(MB4[:, t, :], z12[:, t * P:(t + 1) * P], ident[:, :])
            elif name == "h2T":
                pe.wait_ge(s_x1n, beta + 1)
                for t in range(TB):
                    mm = nc.tensor.transpose(MB4[:, t, :], x1n[:, t, :], ident[:, :])
            elif name[:2] == "l0":
                pe.wait_ge(s_taken["h2T"], beta + 1)
                m = int(name[3])
                mm = nc.tensor.matmul(MB[:, :], W0[:, m * P:(m + 1) * P], h2T[:, :], start=True, stop=True)
            elif name in LONG:
                layer = int(name[1])
                if not second:
                    for m in range(KC):
                        pe.wait_ge(s_taken[f"l{layer - 1}_{m}"], beta + 1)
                for kc in range(KC // 2, KC) if second else range(KC // 2):
                    w = W2[:, kc, :] if layer == 2 else W1[:, kc, int(name[3]) * P:(int(name[3]) + 1) * P]
                    mm = nc.tensor.matmul(MB[:, :], w, hid[layer - 1][:, kc, :], start=(kc == 0), stop=(kc == KC - 1))
                if not second:
                    return
            elif name == "y":
                pe.wait_ge(s_taken["l2"], beta + 1)
                for t in range(TB):
                    mm = nc.tensor.transpose(MB4[:, t, :], z12[:, t * P:(t + 1) * P], ident[:, :])
            mm.then_inc(s_made[name], 1)

        def pe_batch(pe, b):
            def scores(b, n, h):
                if n == H:
                    b, n = b + 1, 0
                if not live(b):
                    return
                if n % QUAD == 0 and h == 0:
                    need(pe, s_mrow[n // QUAD], (b + 1) * PARTS * 16)
                if n:
                    z_taken(pe, b, n - 1, h)
                elif not isinstance(b, int) or b:
                    z_taken(pe, b - 1, H - 1, h)
                for t in range(2):
                    k0_ = (2 * h + t) * P
                    mm = nc.tensor.matmul(Z[:, h, t * S:(t + 1) * S], KH[:, n, k0_:k0_ + P], QH[:, n, :],
                                          start=True, stop=True)
                mm.then_inc(s_z, 1)

            def logits(n, qts):
                beta, g = (b, n // QUAD + 2) if n < 8 else (b + 1, n // QUAD - 2)
                if not live(beta):
                    return
                hh = QUAD * g + n % QUAD
                if n % QUAD == 0 and qts[0] == 0:
                    need(pe, s_qk[g], (beta + 1) * 2 * PARTS * PARTS * 16)
                for qt in qts:
                    i = 64 * beta + TB * hh + qt
                    need(pe, s_mx, i - 1)
                    nc.tensor.matmul(SA[:, qt % 2, :], QH[0:MROW, hh, qt * P:(qt + 1) * P], KH[0:MROW, hh, :],
                                     start=True, stop=True).then_inc(s_a, 1)

            def with_v(n):
                q = (n - LAG) // QUAD - 1
                tb = (n - LAG) % QUAD
                beta, g = (b, q) if q >= 0 else (b - 1, q + NQ)
                if not live(beta):
                    return
                if tb == 0:
                    need(pe, s_p, H * beta + QUAD * g + QUAD)
                    need(pe, s_vq, NQ * beta + g + 1)
                    need(pe, s_ot, NQ * beta + g)
                for j in range(QUAD):
                    hh = QUAD * g + j
                    mm = nc.tensor.matmul(OP[32 * j:32 * j + 2 * HD, :], Vq[:, tb, hh, :],
                                          prob[:, hh % P_RING, tb * S:(tb + 1) * S],
                                          start=(tb == 0), stop=(tb == TB - 1), skip_group_check=True)
                mm.then_inc(s_pv, 1)

            for n in range(H):
                logits(n, (0, 1))
                with_v(n)
                misc_at(pe, b, n, 0)
                scores(b, n + 1, 0)
                logits(n, (2, 3))
                misc_at(pe, b, n, 1)
                scores(b, n + 1, 1)

        def misc_at(pe, b, n, place):
            for i, m in enumerate(MISC):
                if m[:2] == (n, place):
                    misc_product(pe, b, i)
                elif place and m[0] == n and m[2] in LONG:
                    misc_product(pe, b, i, second=True)

        @block.tensor
        def _(pe):
            pe_setup(pe)
            batches(lambda b: pe_batch(pe, b))(nc.tensor)

        def act_setup(act):
            nc.scalar.preload_act_table_set("natural_log_exp_and_others")
            act.wait_ge(s_ld, LOADS * 16)
            nc.scalar.activation(c_exp, c_rows, ACT.Exp, scale=-1.0).then_inc(s_su_a, 1)
            act.wait_ge(s_su_v, 1)
            act.wait_ge(s_one, 2)
            ones = KH[MROW:MROW + PARTS, :, :]
            nc.scalar.activation(ones, ones, ACT.Identity, bias=1.0).then_inc(s_ones_k, 1)

        def act_batch(act, b):
            def from_z(n, h):
                if not live(b) or PATHS[n][h] == "V":
                    return
                need(act, s_z, 2 * H * b + 2 * n + h + 1)
                if PATHS[n][h] == "D":
                    i = before("D", n, h)
                    need(act, s_cv, b * N_D + i - 2)
                    nc.scalar.activation(sq[:, (i - 1) % 2, :], Z[:, h, :], ACT.Square)\
                        .then_inc(s_sq, 1)
                else:
                    i = before("AV", n, h)
                    need(act, s_cp, b * N_P + i - 2)
                    nc.scalar.activation(zc[:, (i - 1) % 2, :], Z[:, h, :], ACT.Copy).then_inc(s_za, 1)

            def log_of(n):
                beta, m = (b, n - 1) if n else (b - 1, H - 1)
                if live(beta):
                    cubic_ready(act, beta, m, 0)
                    cubic_ready(act, beta, m, 1)
                    nc.scalar.activation(cub[:, m % F_RING], cub[:, m % F_RING], ACT.Ln, scale=-1.0,
                                         bias=2.0).then_inc(s_ln, 1)

            def exp_of(n):
                beta, m = (b, n - 1) if n else (b - 1, H - 1)
                if live(beta):
                    need(act, s_ln, H * beta + m + 1)
                    need(act, s_pv, QUAD * (NQ * beta + m // QUAD - 1))
                    nc.scalar.activation(prob[:, m % P_RING, :], cub[:, m % F_RING].rearrange("p a n -> p (a n)"),
                                         ACT.Exp, scale=-1.0).then_inc(s_p, 1)

            def misc(n, place):
                def at(step, where, beta):
                    return (n, place) == (step, where) and live(beta)

                if at(0, 0, b + 1):
                    act.wait_ge(s_made["hT"], b + 2)
                    need(act, s_made["v"], b + 1)
                    nc.scalar.activation(hT[:, :], MB[:, :], ACT.Identity, scale=col(1, b + 1), bias=col(0, b + 1))\
                        .then_inc(s_taken["hT"], 1)
                for i, (step, name, dst) in enumerate(((1, "q", SQ), (2, "k", SK))):
                    if at(step, 0, b + 1):
                        act.wait_ge(s_made[name], b + 2)
                        for g in range(NQ):
                            need(act, s_qk[g], (b + 1) * 2 * PARTS * PARTS * 16)
                        nc.scalar.activation(dst[:, 0, :], MB[:, :], ACT.Copy, scale=SCALE if name == "q" else 1.0)\
                            .then_inc(s_part1, 1)
                if at(3, 0, b - 2):
                    act.wait_ge(s_made["h2T"], b - 1)
                    need(act, s_made["l0_3"], b - 2)
                    nc.scalar.activation(h2T[:, :], MB[:, :], ACT.Identity, scale=col(4, b - 2), bias=col(3, b - 2))\
                        .then_inc(s_taken["h2T"], 1)
                if at(7, 1, b - 1):
                    for g in range(2):
                        act.wait_ge(s_gat[g], b * NQ * QUAD * 16)
                    nc.scalar.activation(den[:, :], den[:, :], ACT.Ln).then_inc(s_dln, 1)
                if at(8, 0, b - 1):
                    act.wait_ge(s_dln, b)
                    nc.scalar.activation(den[:, :], den[:, :], ACT.Exp, scale=-1.0).then_inc(s_dinv, 1)
                if at(9, 0, b + 2):
                    act.wait_ge(s_mv1, b + 3)
                    need(act, s_xn, b + 2)
                    nc.scalar.activation(rs1[:, :], mv1[:, :, 1], ACT.Ln, bias=epst[:, 0:1]).then_inc(s_ln1, 1)
                if at(9, 1, b + 2):
                    act.wait_ge(s_ln1, b + 3)
                    nc.scalar.activation(rs1[:, :], rs1[:, :], ACT.Exp, scale=-0.5).then_inc(s_rs1, 1)
                if at(13, 1, b - 1):
                    act.wait_ge(s_mv2, b)
                    need(act, s_x1n, b - 1)
                    nc.scalar.activation(rs2[:, :], mv2[:, :, 1], ACT.Ln, bias=epst[:, 0:1]).then_inc(s_ln2, 1)
                if at(14, 0, b - 1):
                    act.wait_ge(s_ln2, b)
                    nc.scalar.activation(rs2[:, :], rs2[:, :], ACT.Exp, scale=-0.5).then_inc(s_rs2, 1)

            for n in range(H):
                from_z(n, 0)
                log_of(n)
                misc(n, 0)
                from_z(n, 1)
                exp_of(n)
                misc(n, 1)

        @block.scalar
        def _(act):
            act_setup(act)
            batches(lambda b: act_batch(act, b))(nc.scalar)

        def dve_setup(dve):
            nc.vector.memset(epst[:, :], EPS).then_inc(s_su_v, 1)
            nc.vector.memset(OP[:, :], 0.0)
            dve.wait_ge(s_ld, LOADS * 16)
            nc.vector.tensor_tensor(W0[:, :], k0u[:, 0, :], k0u[:, 1, :], ALU.subtract).then_inc(s_su_v, 1)
            nc.vector.tensor_scalar(W1[:, :, :], k1u, 2.0, -1.0, ALU.mult, ALU.add)
            nc.vector.tensor_scalar(W2[:, :, :], k2u, 2.0, -1.0, ALU.mult, ALU.add)
            dve.wait_ge(s_su_v, 2)
            nc.vector.tensor_scalar(W0[:, :], W0[:, :], 2.0, None, ALU.mult).then_inc(s_su_v, 1)
            dve.wait_ge(s_su_a, 1)
            nc.vector.tensor_scalar(c_exp, c_exp, 1.0, None, ALU.add).then_inc(s_su_v, 1)
            dve.wait_ge(s_su_v, 4)
            nc.vector.reciprocal(c_inv, c_exp).then_inc(s_su_v, 1)
            dve.wait_ge(s_su_v, 5)
            nc.vector.tensor_tensor(c_sil, c_rows, c_inv, ALU.mult).then_inc(s_su_v, 1)
            dve.wait_ge(s_su_pe, 1)
            for i, w in enumerate((wq, wk)):
                nc.vector.tensor_copy(w[:, :].rearrange("p (g d j) -> p g d j", g=NQ, d=HD),
                                      MB4[:, i, :].rearrange("p (g j d) -> p g d j", g=NQ, d=HD))\
                    .then_inc(s_su_v, 1)
            nc.vector.tensor_copy(wv[:, :], MB4[:, 2, :])
            nc.vector.tensor_copy(wo[:, :], MB4[:, 3, :]).then_inc(s_su_v, 1)
            dve.wait_ge(s_su_pe, 2)
            nc.vector.tensor_copy(csil, MB[:, 0:B]).then_inc(s_su_v, 1)
            dve.wait_ge(s_su_pe, 3)
            M6 = MB[:, 64:64 + 6 * B].rearrange("p (i b) -> p i b", i=6)
            nc.vector.tensor_copy(mod[:, 0:6, :], M6).then_inc(s_su_v, 1)
            dve.wait_ge(s_su_v, 11)
            for i in (1, 4):
                nc.vector.tensor_scalar(mod[:, i, :], mod[:, i, :], 1.0, None, ALU.add)
            for n, i in enumerate((2, 5)):
                nc.vector.tensor_scalar(gtmp[:, 0, :], mod[:, i, :], 0.0, 2.0, ALU.is_ge, ALU.mult)
                nc.vector.tensor_scalar(gtmp[:, 1, :], mod[:, i, :], -1.0, None, ALU.mult).then_inc(s_su_v, 1)
                dve.wait_ge(s_su_v, 12 + 3 * n)
                nc.vector.tensor_tensor(gtmp[:, 2, :], gtmp[:, 1, :], mod[:, i, :], ALU.max).then_inc(s_su_v, 1)
                dve.wait_ge(s_su_v, 13 + 3 * n)
                nc.vector.tensor_scalar(gtmp[:, 2, :], gtmp[:, 2, :], 0.25, None, ALU.max)
                nc.vector.tensor_scalar(gtmp[:, 0, :], gtmp[:, 0, :], -1.0, None, ALU.add).then_inc(s_su_v, 1)
                dve.wait_ge(s_su_v, 14 + 3 * n)
                nc.vector.tensor_tensor(mod[:, i, :], gtmp[:, 0, :], gtmp[:, 2, :], ALU.mult).then_inc(s_su_g, 1)
                dve.wait_ge(s_su_g, n + 1)
            nc.vector.tensor_scalar(mod[:, 5, :], mod[:, 5, :], sv[:, 2:3], None, ALU.mult)
            nc.vector.tensor_scalar(mod[:, 6, :], mod[:, 2, :], bo[:, 0:1], None, ALU.mult).then_inc(s_su_v, 1)
            nc.vector.tensor_scalar(sv[:, 0:2], sv[:, 0:2], 2.0, None, ALU.mult).then_inc(s_su_v, 1)
            dve.wait_ge(s_su_v, 19)

        def dve_batch(dve, b):
            def from_z(n, h):
                if not live(b) or PATHS[n][h] == "A":
                    return
                if PATHS[n][h] == "D":
                    i = before("D", n, h)
                    need(dve, s_sq, b * N_D + i)
                    need(dve, s_p, H * b + n + 1 - F_RING)
                    nc.vector.scalar_tensor_tensor(cub[:, n % F_RING, h, :], sq[:, (i - 1) % 2, :], 3.0, Z[:, h, :],
                                                   ALU.add, ALU.mult).then_inc(s_cv, 1)
                else:
                    i = before("AV", n, h)
                    need(dve, s_z, 2 * H * b + 2 * n + h + 1)
                    need(dve, s_cp, b * N_P + i - 2)
                    nc.vector.tensor_copy(zc[:, (i - 1) % 2, :], Z[:, h, :]).then_inc(s_zv, 1)

            def maxima(n, qts):
                beta, g = (b, n // QUAD + 2) if n < 8 else (b + 1, n // QUAD - 2)
                if not live(beta):
                    return
                j = n % QUAD
                for qt in qts:
                    need(dve, s_a, 64 * beta + TB * (QUAD * g + j) + qt + 1)
                    if j == 0 and qt == 0:
                        gg = (g + 2) % NQ
                        name = f"mT{(gg - 1) % NQ}"
                        need(dve, s_made[name], beta if g < 2 else beta + 1)
                    nc.vector.tensor_reduce(mx[:, g % 2, j * TB + qt:j * TB + qt + 1], SA[:, qt % 2, :], AX_X, ALU.max)\
                        .then_inc(s_mx, 1)

            def relu_of(name, beta):
                layer, m = int(name[1]), int(name[3])
                dve.wait_ge(s_made[name], beta + 1)
                last = "l1_3" if layer == 0 else "l2"
                if m == 0:
                    need(dve, s_made[last], beta)
                nc.vector.tensor_scalar(hid[layer][:, m, :], MB[:, :], sv[:, layer:layer + 1], 0.0, ALU.mult, ALU.max)\
                    .then_inc(s_taken[name], 1)

            def misc(n, place):
                def at(step, where, beta):
                    return (n, place) == (step, where) and live(beta)

                for g, (step, beta) in enumerate(((0, b), (4, b), (8, b), (12, b + 1))):
                    if at(step, 1, beta):
                        gg = (g + 1) % NQ
                        dve.wait_ge(s_made[f"mT{g}"], beta + 1)
                        need(dve, s_mp, 4 * (NQ * beta + gg))
                        nc.vector.tensor_scalar(ms[:, :], MB[0:QUAD * TB, 0:P], -1.0, -1.0, ALU.mult, ALU.add)\
                            .then_inc(s_taken[f"mT{g}"], 1)
                for i, (step, name, src, scale) in enumerate(((1, "q", SQ, SCALE), (2, "k", SK, 1.0))):
                    if at(step, 1, b + 1):
                        dve.wait_ge(s_part1, 2 * (b + 1) + i + 1)
                        need(dve, s_part3, 2 * b + i + 1)
                        nc.vector.scalar_tensor_tensor(rem[:, i, :], MB[:, :], scale, src[:, 0, :],
                                                       ALU.mult, ALU.subtract).then_inc(s_taken[name], 1)
                for step, where, name in ((3, 1, "l0_0"), (4, 0, "l0_1"), (5, 0, "l0_2"), (5, 1, "l0_3"),
                                          (6, 1, "l1_0"), (7, 1, "l1_1"), (9, 1, "l1_2"), (11, 1, "l1_3")):
                    if at(step, where, b - 2):
                        relu_of(name, b - 2)
                if n % QUAD == (LAG + QUAD - 1) % QUAD and place == 1:
                    q = (n - LAG) // QUAD - 1
                    beta, g = (b, q) if q >= 0 else (b - 1, q + NQ)
                    if live(beta):
                        i = NQ * beta + g
                        dve.wait_ge(s_pv, QUAD * (i + 1))
                        need(dve, s_gat[g % 2], (2 * beta + g // 2) * 2 * QUAD * 16)
                        nc.vector.tensor_copy(OT[:, g % 2, :], OP[:, :]).then_inc(s_ot, 1)
                if at(6, 0, b + 2):
                    dve.wait_ge(s_xa, 16 * (b + 3))
                    for t in range(TB):
                        bn = nc.vector.bn_stats(st1[:, t, :], xa[:, t, :])
                    bn.then_inc(s_st1, 1)
                if at(7, 1, b + 2):
                    dve.wait_ge(s_st1, b + 3)
                    need(dve, s_xn, b + 2)
                    apart(dve, b)
                    for t in range(TB):
                        bn = nc.vector.bn_aggr(mv1[:, t, :], st1[:, t, :])
                    bn.then_inc(s_mv1, 1)
                if at(10, 0, b - 1):
                    dve.wait_ge(s_made["proj"], b)
                    need(dve, s_made["y"], b - 2)
                    nc.vector.tensor_scalar(z12[:, :], MB[:, :], col(2, b - 1), col(6, b - 1), ALU.mult, ALU.add)\
                        .then_inc(s_taken["proj"], 1)
                if at(10, 1, b - 1):
                    dve.wait_ge(s_made["x1"], b)
                    dve.wait_ge(s_xb, 16 * b)
                    need(dve, s_x1k, b - 1)
                    need(dve, s_x1n, b - 1)
                    nc.vector.tensor_tensor(x1[:, :, :], MB4, xb[:, :, :], ALU.add).then_inc(s_taken["x1"], 1)
                if at(11, 0, b - 1):
                    dve.wait_ge(s_taken["x1"], b)
                    for t in range(TB):
                        bn = nc.vector.bn_stats(st2[:, t, :], x1[:, t, :])
                    bn.then_inc(s_st2, 1)
                if at(12, 0, b - 1):
                    dve.wait_ge(s_st2, b)
                    need(dve, s_x1n, b - 1)
                    apart(dve, b)
                    for t in range(TB):
                        bn = nc.vector.bn_aggr(mv2[:, t, :], st2[:, t, :])
                    bn.then_inc(s_mv2, 1)
                if at(13, 1, b - 2):
                    dve.wait_ge(s_made["l2"], b - 1)
                    need(dve, s_made["x1"], min(b, B) if isinstance(b, int) else b)
                    nc.vector.tensor_scalar(z12[:, :], MB[:, :], col(5, b - 2), None, ALU.mult)\
                        .then_inc(s_taken["l2"], 1)
                if at(12, 0, b + 1):
                    dve.wait_ge(s_made["v"], b + 2)
                    need(dve, s_vq, NQ * (b + 1))
                    nc.vector.tensor_copy(Vn[:, :, :, :].rearrange("p t h d -> p t (h d)"), MB4)\
                        .then_inc(s_taken["v"], 1)
                if at(14, 0, b - 2):
                    dve.wait_ge(s_made["y"], b - 1)
                    need(dve, s_x1k, b - 1)
                    need(dve, s_out, 16 * (b - 2))
                    nc.vector.tensor_tensor(y[:, :, :], MB4, x1k[:, :, :], ALU.add).then_inc(s_taken["y"], 1)

            for n in range(H):
                from_z(n, 0)
                maxima(n, (0, 1))
                misc(n, 0)
                from_z(n, 1)
                maxima(n, (2, 3))
                misc(n, 1)

        @block.vector
        def _(dve):
            dve_setup(dve)
            batches(lambda b: dve_batch(dve, b))(nc.vector)

        def pool_setup(pool):
            nc.gpsimd.memset(ident[:, :], 0.0).then_inc(s_id, 1)
            pool.wait_ge(s_id, 1)
            nc.gpsimd.affine_select(out=ident[:, :], in_=ident[:, :], compare_op=ALU.not_equal, fill=1.0, base=0,
                                    pattern=[[-1, P]], channel_multiplier=1).then_inc(s_id, 1)
            for t in (QH, KH):
                nc.gpsimd.memset(t[:, :, :].bitcast(F32), 0.0).then_inc(s_one, 1)
            nc.gpsimd.memset(Vq[:, :, :, HD:2 * HD], 1.0).then_inc(s_one, 1)

        def pool_batch(pool, b):
            def from_z(n, h):
                if not live(b) or PATHS[n][h] == "D":
                    return
                i = before("AV", n, h)
                if PATHS[n][h] == "A":
                    need(pool, s_za, b * N_A + before("A", n, h))
                else:
                    need(pool, s_zv, b * N_V + before("V", n, h))
                need(pool, s_p, H * b + n + 1 - F_RING)
                zz, cc = zc[:, (i - 1) % 2, :], cub[:, n % F_RING, h, :]
                nc.gpsimd.tensor_tensor(cc, zz, zz, ALU.mult).then_inc(s_q1, 1)
                need(pool, s_q1, 2 * (b * N_P + i) - 1)
                apart(pool, b)
                nc.gpsimd.tensor_scalar(cc, cc, 1.0, 3.0, ALU.mult, ALU.add).then_inc(s_q1, 1)
                need(pool, s_q1, 2 * (b * N_P + i))
                nc.gpsimd.tensor_tensor(cc, cc, zz, ALU.mult).then_inc(s_cp, 1)

            def normalise(beta, src, mv, rs, dst, s_rs, s_free, s_done, free):
                pool.wait_ge(s_rs, beta + 1)
                need(pool, s_free, free)
                apart(pool, beta)
                for t in range(TB):
                    last = nc.gpsimd.tensor_scalar(dst[:, t, :], src[:, t, :], mv[:, t, 0:1], rs[:, t:t + 1],
                                                   ALU.subtract, ALU.mult)
                last.then_inc(s_done, 1)

            def v_in(beta, g):
                if live(beta):
                    i = NQ * beta + g
                    pool.wait_ge(s_taken["v"], beta + 1)
                    need(pool, s_pv, QUAD * (i + 1 - NQ))
                    apart(pool, beta)
                    hs = slice(QUAD * g, QUAD * (g + 1))
                    nc.gpsimd.tensor_copy(Vq[:, :, hs, 0:HD], Vn[:, :, hs, :]).then_inc(s_vq, 1)

            def misc(n, place):
                def at(step, where, beta):
                    return (n, place) == (step, where) and live(beta)

                for i, (step, dst) in enumerate(((2, SQ), (3, SK))):
                    if at(step, 0, b + 1):
                        k = 2 * (b + 1) + i + 1
                        pool.wait_ge(s_taken["qk"[i]], b + 2)
                        apart(pool, b)
                        nc.gpsimd.tensor_scalar(dst[:, 1, :], rem[:, i, :], 1.0, 0.0, ALU.mult, ALU.add)\
                            .then_inc(s_part2, 1)
                        pool.wait_ge(s_part2, k)
                        nc.gpsimd.tensor_tensor(dst[:, 2, :], rem[:, i, :], dst[:, 1, :], ALU.subtract)\
                            .then_inc(s_part3, 1)
                for g, (step, beta) in enumerate(((1, b), (5, b), (9, b), (13, b + 1))):
                    if at(step, 0, beta):
                        gg = (g + 1) % NQ
                        k = 4 * (NQ * beta + gg)
                        pool.wait_ge(s_taken[f"mT{g}"], beta + 1)
                        need(pool, s_mrow[(gg - 1) % NQ], (beta + (gg > 0)) * PARTS * 16)
                        apart(pool, b)
                        nc.gpsimd.tensor_scalar(mp[:, 0, :], ms[:, :], 1.0, 0.0, ALU.mult, ALU.add).then_inc(s_mp, 1)
                        pool.wait_ge(s_mp, k + 1)
                        nc.gpsimd.tensor_tensor(mrem[:, :], ms[:, :], mp[:, 0, :], ALU.subtract)\
                            .then_inc(s_mp, 1)
                        pool.wait_ge(s_mp, k + 2)
                        apart(pool, b)
                        nc.gpsimd.tensor_scalar(mp[:, 1, :], mrem[:, :], 1.0, 0.0, ALU.mult, ALU.add).then_inc(s_mp, 1)
                        pool.wait_ge(s_mp, k + 3)
                        nc.gpsimd.tensor_tensor(mp[:, 2, :], mrem[:, :], mp[:, 1, :], ALU.subtract)\
                            .then_inc(s_mp, 1)
                if at(8, 1, b - 1):
                    pool.wait_ge(s_dinv, b)
                    nc.gpsimd.tensor_tensor(num[:, :], num[:, :], den[:, :], ALU.mult)\
                        .then_inc(s_att, 1)
                if at(10, 1, b + 2):
                    normalise(b + 2, xa, mv1, rs1, xn, s_rs1, s_made["hT"], s_xn, b + 2)
                if at(0, 0, b - 2) :
                    pool.wait_ge(s_taken["x1"], b - 1)
                    need(pool, s_taken["y"], b - 2)
                    apart(pool, b)
                    nc.gpsimd.tensor_scalar(x1k[:, :, :], x1[:, :, :], 1.0, 0.0, ALU.mult, ALU.add).then_inc(s_x1k, 1)
                if at(14, 1, b - 1):
                    normalise(b - 1, x1, mv2, rs2, x1n, s_rs2, s_made["h2T"], s_x1n, b - 1)
                if (n, place) == (3, 1):
                    v_in(b, 2)
                if (n, place) == (6, 0):
                    v_in(b, 3)
                if (n, place) == (15, 1):
                    v_in(b + 1, 0)
                    v_in(b + 1, 1)

            for n in range(H):
                from_z(n, 0)
                misc(n, 0)
                from_z(n, 1)
                misc(n, 1)

        @block.gpsimd
        def _(pool):
            pool_setup(pool)
            batches(lambda b: pool_batch(pool, b))(nc.gpsimd)

        def sp_setup(sp):
            sp.dma_start(w_rows[:, 0:3, :], w_qkv.rearrange("(k p) d -> p k d", p=P)).then_inc(s_ld, 16)
            sp.dma_start(w_rows[:, 3, :], w_out).then_inc(s_ld, 16)
            sp.dma_start(c_rows, c).then_inc(s_ld, 16)
            sp.dma_start(wm, wmod).then_inc(s_ld, 16)
            sp.dma_start(k0u, k0.rearrange("(a p) n -> p a n", p=P)).then_inc(s_ld, 16)
            sp.dma_start(k1u, k1.rearrange("(a p) n -> p a n", p=P)).then_inc(s_ld, 16)
            sp.dma_start(k2u, k2.rearrange("(a p) n -> p a n", p=P)).then_inc(s_ld, 16)
            sp.dma_start(bo[:, :], b_out.rearrange("(d a) -> d a", a=1)).then_inc(s_ld, 16)
            for i, s in enumerate((s0, s1, s2)):
                sp.dma_start(sv[:, i:i + 1], s.partition_broadcast(P)).then_inc(s_ld, 16)

        def sp_need(sp, b, s, n):
            need(sp, s, n)
            apart(sp, b)

        def sp_batch(sp, b):
            for g in range(NQ):
                beta, gg = (b, NQ - 1) if g == 0 else (b + 1, g - 1)
                if live(beta):
                    sp_need(sp, b, s_part3, 2 * beta + 2)
                    sp_need(sp, b, s_z, 2 * QUAD * (NQ * (beta - 1) + gg + 1))
                    if isinstance(beta, int) and beta == 0 and gg == 0:
                        sp.wait_ge(s_one, 2)
                    rows = slice(32 * gg, 32 * gg + 32)
                    heads = slice(QUAD * gg, QUAD * gg + QUAD)
                    for a in range(PARTS):
                        for c_ in range(PARTS):
                            r = (PARTS * a + c_) * HD
                            sp.dma_start(QH[r:r + HD, heads, :], SQ[rows, a, :]).then_inc(s_qk[gg], 16)
                            sp.dma_start(KH[r:r + HD, heads, :], SK[rows, c_, :]).then_inc(s_qk[gg], 16)
                if g == 0 and live(b + 2):
                    sp_need(sp, b, s_xn, b + 2)
                    sp.dma_start(xa[:, :, :], x_t[:, bass.ds((b + 2) * TB, TB), :]).then_inc(s_xa, 16)
                beta, gg = (b, g + 1) if g < NQ - 1 else (b + 1, 0)
                if live(beta):
                    sp_need(sp, b, s_mp, 4 * (NQ * beta + gg + 1))
                    for a in range(PARTS):
                        sp.dma_start(QH[MROW + a:MROW + a + 1, QUAD * gg:QUAD * gg + QUAD, :], mp[:, a, :])\
                            .then_inc(s_mrow[gg], 16)
                if g == 2 and live(b - 1):
                    sp_need(sp, b, s_taken["x1"], b - 1)
                    sp.dma_start(xb[:, :, :], x_t[:, bass.ds((b - 1) * TB, TB), :]).then_inc(s_xb, 16)
                beta, gg = (b, g - 2) if g >= 2 else (b - 1, g + 2)
                if live(beta):
                    sp_need(sp, b, s_ot, NQ * beta + gg + 1)
                    if gg == 0:
                        sp_need(sp, b, s_made["proj"], beta)
                    for j in range(QUAD):
                        r = 32 * gg + HD * j
                        sp.dma_start(num[r:r + HD, :], OT[32 * j:32 * j + HD, gg % 2, :]).then_inc(s_gat[gg % 2], 16)
                        sp.dma_start(den[r:r + HD, :], OT[32 * j + HD:32 * j + 2 * HD, gg % 2, :]).then_inc(s_gat[gg % 2], 16)
                if g == 3 and live(b - 2):
                    sp_need(sp, b, s_taken["y"], b - 1)
                    sp.dma_start(out_t[:, bass.ds((b - 2) * TB, TB), :], y[:, :, :]).then_inc(s_out, 16)

        @block.sync
        def _(sp):
            sp_setup(sp)
            batches(lambda b: sp_batch(sp, b))(nc.sync)
            sp.wait_ge(s_out, 16 * B)


_INS = ["L0_attn_x", "L0_attn_w_qkv", "L0_attn_w_out", "L0_attn_b_out", "L0_ffn_k0", "L0_ffn_k1", "L0_ffn_k2",
        "L0_ffn_s0", "L0_ffn_s1", "L0_ffn_s2", "L0_c", "L0_wmod"]


def kernel(**inputs):
    import numpy as np
    import concourse.bacc as bacc
    from concourse.bass_utils import run_bass_kernel_spmd

    nc = bacc.Bacc("TRN2", target_bir_lowering=False, num_devices=1)
    arrays, args = {}, []
    for name in _INS:
        a = np.ascontiguousarray(inputs[name])
        if a.ndim == 0:
            a = a.reshape(1)
        arrays[name] = a
        args.append(nc.dram_tensor(name, a.shape, mybir.dt.from_np(a.dtype), kind="ExternalInput").ap())
    out = nc.dram_tensor("out", (B, S, D), F32, kind="ExternalOutput").ap()
    adaln_block(nc, *args, out)
    r = run_bass_kernel_spmd(nc, [arrays], core_ids=[0])
    return r.results[0]["out"]
```

```python
from contextlib import ExitStack

import concourse.bass as bass
from concourse import mybir

F32 = mybir.dt.float32
BF16 = mybir.dt.bfloat16
U8 = mybir.dt.uint8
ALU = mybir.AluOpType
ACT = mybir.ActivationFunctionType
AX_X = mybir.AxisListType.X

P = 128
B = 8
S = 512
D = 128
H = 16
HD = D // H
QUAD = 4
NQ = H // QUAD
TB = S // P
HALF = 2 * S
F = 512
KC = F // P
PARTS = 3
NROW = PARTS * PARTS * HD
MROW = 96
EPS = 1e-5
E_DMAS = PARTS + 1
SCALE = HD ** -0.5


PATHS = [("D", "D") for n in range(H)]
P_RING = 8
F_RING = 2

LAG = 2


def before(kinds, n, h):
    return sum(PATHS[m][k] in kinds for m in range(H) for k in range(2) if (m, k) <= (n, h))


N_D = before("D", H, 0)
N_A = before("A", H, 0)
N_V = before("V", H, 0)
N_P = N_A + N_V
assert N_D % 2 == 0 and N_P % 2 == 0

MISC = [
    (0, "hT", 1), (1, "q", 1), (2, "k", 1), (3, "h2T", -2), (4, "l0_0", -2), (5, "l0_1", -2), (6, "l0_2", -2),
    (7, "l0_3", -2), (8, "l1_0", -2), (9, "l1_1", -2), (10, "x1", -1), (11, "l1_2", -2), (12, "l1_3", -2),
    (13, "v", 1), (14, "y", -2),
]
LONG = ("l1_0", "l1_1", "l1_2", "l1_3", "y")
STEP = {name: step for step, name, _ in MISC}


def live(beta):
    return not isinstance(beta, int) or 0 <= beta < B


def adaln_block(nc, x, w_qkv, w_out, b_out, k0, k1, k2, s0, s1, s2, c, wmod, out):
    x_t = x.rearrange("b (t p) d -> p (b t) d", p=P)
    parts_q = nc.dram_tensor("parts_q", (NQ, PARTS, QUAD * HD, S), BF16, kind="Internal").ap()
    parts_k = nc.dram_tensor("parts_k", (NQ, PARTS, QUAD * HD, S), BF16, kind="Internal").ap()
    gate_rows = nc.dram_tensor("gate_rows", (B, 3 * D), F32, kind="Internal").ap()
    out_t = out.rearrange("b (t p) d -> p (b t) d", p=P)

    with ExitStack() as ctx:
        def sb(name, shape, dt=F32):
            return ctx.enter_context(nc.sbuf_tensor(name, shape, dt))

        def sem(name):
            return ctx.enter_context(nc.semaphore(name))

        Z = ctx.enter_context(nc.psum_tensor("Z", [P, 2, HALF], F32))
        SA = ctx.enter_context(nc.psum_tensor("SA", [P, 2, S], F32))
        OP = ctx.enter_context(nc.psum_tensor("OP", [P, S], F32))
        MB = ctx.enter_context(nc.psum_tensor("MB", [P, S], F32))
        MB4 = MB[:, :].rearrange("p (t d) -> p t d", t=TB)

        QH = sb("QH", [P, H, S], BF16)
        KH = sb("KH", [P, H, S], BF16)
        prob = sb("prob", [P, P_RING, TB * S])
        cub = sb("cub", [P, F_RING, 2, HALF])
        sq = sb("sq", [P, 2, HALF])
        zc = sb("zc", [P, 2, HALF])
        Vq = sb("Vq", [P, TB, H, 2 * HD])
        Vn = sb("Vn", [P, TB, H, HD])
        SQ = sb("SQ", [P, PARTS, S], BF16)
        SK = sb("SK", [P, PARTS, S], BF16)
        rem = sb("rem", [P, 2, S])
        mx = sb("mx", [P, 2, QUAD * TB])
        ms = sb("ms", [QUAD * TB, P])
        mrem = sb("mrem", [QUAD * TB, P])
        mp = sb("mp", [QUAD * TB, PARTS, P], BF16)
        OT = sb("OT", [P, 2, S])
        num = sb("num", [P, S])
        den = sb("den", [P, S])
        xa = sb("xa", [P, TB, D])
        xn = sb("xn", [P, TB, D])
        hT = sb("hT", [P, S])
        xb = sb("xb", [P, TB, D])
        woG = sb("woG", [P, D])
        W2G = sb("W2G", [P, KC, D])
        gA = sb("gA", [P, 2 * D])
        gB = sb("gB", [P, D])
        one = sb("one", [1, P])
        x1 = sb("x1", [P, TB, D])
        x1k = sb("x1k", [P, TB, D])
        x1n = sb("x1n", [P, TB, D])
        h2T = sb("h2T", [P, S])
        hid = [sb("hid0", [P, KC, S]), sb("hid1", [P, KC, S])]
        y = sb("y", [P, TB, D])
        wq = sb("wq", [P, D])
        wk = sb("wk", [P, D])
        wv = sb("wv", [P, D])
        wo = sb("wo", [P, D])
        W0 = sb("W0", [P, F])
        W1 = sb("W1", [P, KC, F])
        W2 = sb("W2", [P, KC, D])
        ident = sb("ident", [P, P])
        mod = sb("mod", [P, 4, B])
        sv = sb("sv", [P, 3])
        st1 = sb("st1", [P, TB, 6])
        mv1 = sb("mv1", [P, TB, 2])
        rs1 = sb("rs1", [P, TB])
        st2 = sb("st2", [P, TB, 6])
        mv2 = sb("mv2", [P, TB, 2])
        rs2 = sb("rs2", [P, TB])
        epst = sb("epst", [P, 1])

        stage = prob[:, 0, :]
        w_rows = stage[:, 0:4 * D].rearrange("p (k d) -> p k d", k=4)
        wm = stage[:, 512:512 + 6 * D]
        cT = stage[:, 1280:1280 + B]
        csil = stage[:, 1296:1296 + B]
        c_rows = stage[0:B, 1408:1408 + D]
        c_exp = stage[0:B, 1536:1536 + D]
        c_inv = stage[0:B, 1664:1664 + D]
        c_sil = stage[0:B, 1792:1792 + D]
        side = prob[0:B, 2, :]
        g_in = side[:, 0:2 * D]
        g_sign = side[:, 256:256 + 2 * D]
        g_abs = side[:, 512:512 + 2 * D]
        g_row = side[:, 768:768 + 3 * D]
        bo8 = side[:, 1280:1280 + D]
        k_u8 = prob[:, 1, :].bitcast(U8)
        k0u = k_u8[:, 0:2 * F].rearrange("p (a n) -> p a n", a=2)
        k1u = k_u8[:, 1024:1024 + KC * F].rearrange("p (a n) -> p a n", a=KC)
        k2u = k_u8[:, 4096:4096 + KC * D].rearrange("p (a n) -> p a n", a=KC)

        ld_c = sem("ld_c")
        ld_w = sem("ld_w")
        ld_s = sem("ld_s")
        ld_k = sem("ld_k")
        s_id = sem("s_id")
        s_apart = sem("s_apart")
        s_eps = sem("s_eps")
        s_cexp = sem("s_cexp")
        s_silu = sem("s_silu")
        s_csT = sem("s_csT")
        s_csil = sem("s_csil")
        s_wT = sem("s_wT")
        s_wcp = sem("s_wcp")
        s_modp = sem("s_modp")
        s_mod = sem("s_mod")
        s_gate = sem("s_gate")
        s_gw = sem("s_gw")
        s_sv = sem("s_sv")
        s_wts = sem("s_wts")
        s_W0 = sem("s_W0")
        s_gA = sem("s_gA")
        s_gB = sem("s_gB")
        s_wog = sem("s_wog")
        s_w2g = sem("s_w2g")
        s_parts = sem("s_parts")
        s_z = sem("s_z")
        s_sq = sem("s_sq")
        s_za = sem("s_za")
        s_zv = sem("s_zv")
        s_cv = sem("s_cv")
        s_q1 = sem("s_q1")
        s_cp = sem("s_cp")
        s_ln = sem("s_ln")
        s_p = sem("s_p")
        s_pv = sem("s_pv")
        s_a = sem("s_a")
        s_mx = sem("s_mx")
        s_mt = sem("s_mt")
        s_ms = sem("s_ms")
        s_mp = sem("s_mp")
        s_mrow = [sem(f"s_mrow{g}") for g in range(NQ)]
        s_qk = [sem(f"s_qk{g}") for g in range(NQ)]
        s_ot = sem("s_ot")
        s_gat = [sem(f"s_gat{g}") for g in range(2)]
        s_vq = sem("s_vq")
        s_one = sem("s_one")
        s_made = {m[1]: sem("made_" + m[1]) for m in MISC}
        s_taken = {m[1]: sem("taken_" + m[1]) for m in MISC}
        s_part1 = sem("s_part1")
        s_part2 = sem("s_part2")
        s_part3 = sem("s_part3")
        s_xa = sem("s_xa")
        s_xb = sem("s_xb")
        s_st1 = sem("s_st1")
        s_mv1 = sem("s_mv1")
        s_ln1 = sem("s_ln1")
        s_rs1 = sem("s_rs1")
        s_xn = sem("s_xn")
        s_st2 = sem("s_st2")
        s_mv2 = sem("s_mv2")
        s_ln2 = sem("s_ln2")
        s_rs2 = sem("s_rs2")
        s_x1n = sem("s_x1n")
        s_x1k = sem("s_x1k")
        s_dln = sem("s_dln")
        s_dinv = sem("s_dinv")
        s_att = sem("s_att")
        s_out = sem("s_out")

        def need(eng, s, n):
            if not isinstance(n, int) or n > 0:
                eng.wait_ge(s, n)

        def apart(eng, b):
            if not isinstance(b, int):
                eng.sem_inc(s_apart)

        def z_taken(eng, b, n, h):
            kind = PATHS[n][h]
            s, per = {"D": (s_cv, N_D), "A": (s_za, N_A), "V": (s_zv, N_V)}[kind]
            need(eng, s, b * per + before(kind, n, h))

        def cubic_ready(eng, b, n, h):
            if PATHS[n][h] == "D":
                need(eng, s_cv, b * N_D + before("D", n, h))
            else:
                need(eng, s_cp, b * N_P + before("AV", n, h))

        def quad_before(b, n):
            return (b, n // QUAD + 1) if n // QUAD < NQ - 1 else (b + 1, 0)

        def batches(body):
            def run(eng):
                for b in range(-1, 3):
                    body(b)
                with eng.Fori(3, B - 2) as b:
                    body(b)
                for b in range(B - 2, B + 2):
                    body(b)
            return run

        def col(i, b):
            return mod[:, i, bass.ds(b, 1)]

        block = ctx.enter_context(nc.Block())

        def pe_setup(pe):
            pe.wait_ge(s_id, 2)
            pe.wait_ge(s_silu, 3)
            nc.tensor.transpose(MB[:, 0:B], c_sil, ident[0:B, 0:B]).then_inc(s_csT, 1)
            pe.wait_ge(ld_w, 3 * 16)
            for i in range(4):
                mm = nc.tensor.transpose(SA[:, 0, i * D:(i + 1) * D], w_rows[:, i, :], ident[:, :])
            mm.then_inc(s_wT, 1)
            pe.wait_ge(s_csil, 1)
            for n, i in enumerate((0, 1, 3, 4)):
                nc.tensor.matmul(MB[:, 64 + n * B:64 + (n + 1) * B], wm[:, i * D:(i + 1) * D], csil,
                                 start=True, stop=True)
            for n, i in enumerate((2, 5)):
                mm = nc.tensor.matmul(SA[0:B, 1, n * D:(n + 1) * D], csil, wm[:, i * D:(i + 1) * D],
                                      start=True, stop=True)
            mm.then_inc(s_modp, 1)
            pe.wait_ge(s_mod, 1)
            pe.wait_ge(s_wcp, 1)
            pe.wait_ge(s_gate, 1)

        def misc_prev(b, i):
            while True:
                i, b = (i - 1, b) if i else (len(MISC) - 1, b - 1)
                if live(b + MISC[i][2]):
                    return MISC[i][1], b + MISC[i][2]
                if isinstance(b, int) and b < -2:
                    return None

        def misc_product(pe, b, i, second=False):
            _, name, off = MISC[i]
            beta = b + off
            if not live(beta):
                return
            prev = misc_prev(b, i)
            if prev and not second:
                need(pe, s_taken[prev[0]], prev[1] + 1)
            if name == "hT":
                pe.wait_ge(s_xn, beta + 1)
                for t in range(TB):
                    mm = nc.tensor.transpose(MB4[:, t, :], xn[:, t, :], ident[:, :])
            elif name in "qk":
                pe.wait_ge(s_taken["hT"], beta + 1)
                mm = nc.tensor.matmul(MB[:, :], (wq if name == "q" else wk)[:, :], hT[:, :], start=True, stop=True)
            elif name == "v":
                for t in range(TB):
                    mm = nc.tensor.matmul(MB4[:, t, :], hT[:, t * P:(t + 1) * P], wv[:, :], start=True, stop=True)
            elif name == "x1":
                pe.wait_ge(s_att, beta + 1)
                pe.wait_ge(s_wog, beta + 1)
                for t in range(TB):
                    nc.tensor.matmul(MB4[:, t, :], num[:, t * P:(t + 1) * P], woG[:, :], start=True, stop=False)
                    mm = nc.tensor.matmul(MB4[:, t, :], one[:, :], gA[0:1, D:2 * D], start=False, stop=True)
            elif name == "h2T":
                pe.wait_ge(s_x1n, beta + 1)
                for t in range(TB):
                    mm = nc.tensor.transpose(MB4[:, t, :], x1n[:, t, :], ident[:, :])
            elif name[:2] == "l0":
                pe.wait_ge(s_taken["h2T"], beta + 1)
                if isinstance(beta, int) and beta == 0:
                    pe.wait_ge(s_wts, 2)
                    pe.wait_ge(s_W0, 2)
                m = int(name[3])
                mm = nc.tensor.matmul(MB[:, :], W0[:, m * P:(m + 1) * P], h2T[:, :], start=True, stop=True)
            elif name[:2] == "l1":
                if not second:
                    for m in range(KC):
                        pe.wait_ge(s_taken[f"l0_{m}"], beta + 1)
                m = int(name[3])
                for kc in range(KC // 2, KC) if second else range(KC // 2):
                    mm = nc.tensor.matmul(MB[:, :], W1[:, kc, m * P:(m + 1) * P], hid[0][:, kc, :],
                                          start=(kc == 0), stop=(kc == KC - 1))
                if not second:
                    return
            elif name == "y":
                if not second:
                    pe.wait_ge(s_w2g, beta + 1)
                    for m in range(KC):
                        pe.wait_ge(s_taken[f"l1_{m}"], beta + 1)
                for t in range(TB // 2, TB) if second else range(TB // 2):
                    for kc in range(KC):
                        mm = nc.tensor.matmul(MB4[:, t, :], hid[1][:, kc, t * P:(t + 1) * P], W2G[:, kc, :],
                                              start=(kc == 0), stop=(kc == KC - 1))
                if not second:
                    return
            mm.then_inc(s_made[name], 1)

        def pe_batch(pe, b):
            def scores(b, n, h):
                if n == H:
                    b, n = b + 1, 0
                if not live(b):
                    return
                if n % QUAD == 0 and h == 0:
                    need(pe, s_mrow[n // QUAD], (b + 1) * PARTS * 16)
                if n:
                    z_taken(pe, b, n - 1, h)
                elif not isinstance(b, int) or b:
                    z_taken(pe, b - 1, H - 1, h)
                for t in range(2):
                    k0_ = (2 * h + t) * P
                    mm = nc.tensor.matmul(Z[:, h, t * S:(t + 1) * S], KH[:, n, k0_:k0_ + P], QH[:, n, :],
                                          start=True, stop=True)
                mm.then_inc(s_z, 1)

            def logits(n, qts):
                beta, g = (b, n // QUAD + 2) if n < 8 else (b + 1, n // QUAD - 2)
                if not live(beta):
                    return
                hh = QUAD * g + n % QUAD
                if n % QUAD == 0 and qts[0] == 0:
                    need(pe, s_qk[g], (beta + 1) * E_DMAS * 16)
                for qt in qts:
                    i = 64 * beta + TB * hh + qt
                    need(pe, s_mx, i - 1)
                    if n % QUAD == 0 and qt == TB - 1:
                        need(pe, s_ms, NQ * beta + g)
                    nc.tensor.matmul(SA[:, qt % 2, :], QH[0:MROW, hh, qt * P:(qt + 1) * P], KH[0:MROW, hh, :],
                                     start=True, stop=True).then_inc(s_a, 1)

            def maxima_across(n):
                beta, g = quad_before(b, n)
                if n % QUAD or not live(beta):
                    return
                follows = n != 8 or live(b + 1)
                pe.wait_ge(s_mx, TB * H * beta + TB * QUAD * (g + 1) + (2 if follows else 0))
                nc.tensor.transpose(SA[0:QUAD * TB, 1, 0:P], mx[:, g % 2, :], ident[:, :]).then_inc(s_mt, 1)

            def with_v(n):
                q = (n - LAG) // QUAD - 1
                tb = (n - LAG) % QUAD
                beta, g = (b, q) if q >= 0 else (b - 1, q + NQ)
                if not live(beta):
                    return
                if tb == 0:
                    need(pe, s_p, H * beta + QUAD * g + QUAD)
                    need(pe, s_vq, NQ * beta + g + 1)
                    need(pe, s_ot, NQ * beta + g)
                for j in range(QUAD):
                    hh = QUAD * g + j
                    mm = nc.tensor.matmul(OP[32 * j:32 * j + 2 * HD, :], Vq[:, tb, hh, :],
                                          prob[:, hh % P_RING, tb * S:(tb + 1) * S],
                                          start=(tb == 0), stop=(tb == TB - 1), skip_group_check=True)
                mm.then_inc(s_pv, 1)

            for n in range(H):
                logits(n, (0, 1))
                with_v(n)
                misc_at(pe, b, n, 0)
                scores(b, n + 1, 0)
                logits(n, (2,))
                maxima_across(n)
                logits(n, (3,))
                misc_at(pe, b, n, 1)
                scores(b, n + 1, 1)

        def misc_at(pe, b, n, place):
            for i, m in enumerate(MISC):
                if m[0] == n and not place:
                    misc_product(pe, b, i)
                elif m[0] == n and m[1] in LONG:
                    misc_product(pe, b, i, second=True)

        @block.tensor
        def _(pe):
            pe_setup(pe)
            batches(lambda b: pe_batch(pe, b))(nc.tensor)

        def act_setup(act):
            nc.scalar.preload_act_table_set("natural_log_exp_and_others")
            act.wait_ge(ld_c, 16)
            nc.scalar.activation(c_exp, c_rows, ACT.Exp, scale=-1.0).then_inc(s_cexp, 1)
            act.wait_ge(s_eps, 1)
            act.wait_ge(s_mv1, 1)
            nc.scalar.activation(rs1[:, :], mv1[:, :, 1], ACT.Ln, bias=epst[:, 0:1]).then_inc(s_ln1, 1)
            act.wait_ge(s_ln1, 1)
            nc.scalar.activation(rs1[:, :], rs1[:, :], ACT.Exp, scale=-0.5).then_inc(s_rs1, 1)
            act.wait_ge(s_mod, 3)

        def act_batch(act, b):
            def from_z(n, h):
                if not live(b) or PATHS[n][h] == "V":
                    return
                need(act, s_z, 2 * H * b + 2 * n + h + 1)
                if PATHS[n][h] == "D":
                    i = before("D", n, h)
                    need(act, s_cv, b * N_D + i - 2)
                    nc.scalar.activation(sq[:, (i - 1) % 2, :], Z[:, h, :], ACT.Square)\
                        .then_inc(s_sq, 1)
                else:
                    i = before("AV", n, h)
                    need(act, s_cp, b * N_P + i - 2)
                    nc.scalar.activation(zc[:, (i - 1) % 2, :], Z[:, h, :], ACT.Copy).then_inc(s_za, 1)

            def log_of(n):
                beta, m = (b, n - 1) if n else (b - 1, H - 1)
                if live(beta):
                    cubic_ready(act, beta, m, 0)
                    cubic_ready(act, beta, m, 1)
                    nc.scalar.activation(cub[:, m % F_RING], cub[:, m % F_RING], ACT.Ln, scale=-1.0,
                                         bias=2.0).then_inc(s_ln, 1)

            def exp_of(n):
                beta, m = (b, n - 1) if n else (b - 1, H - 1)
                if live(beta):
                    need(act, s_ln, H * beta + m + 1)
                    if isinstance(beta, int) and beta == 0 and m == 0:
                        act.wait_ge(s_wts, 2)
                        act.wait_ge(s_W0, 2)
                        act.wait_ge(s_gw, 16)
                    need(act, s_pv, QUAD * (NQ * beta + m // QUAD - 1))
                    nc.scalar.activation(prob[:, m % P_RING, :], cub[:, m % F_RING].rearrange("p a n -> p (a n)"),
                                         ACT.Exp, scale=-1.0).then_inc(s_p, 1)

            def misc(n, place):
                def at(step, where, beta):
                    return (n, place) == (step, where) and live(beta)

                if at(STEP["hT"], 1, b + 1):
                    act.wait_ge(s_made["hT"], b + 2)
                    need(act, s_made["v"], b + 1)
                    nc.scalar.activation(hT[:, :], MB[:, :], ACT.Identity, scale=col(1, b + 1), bias=col(0, b + 1))\
                        .then_inc(s_taken["hT"], 1)
                for name, dst in (("q", SQ), ("k", SK)):
                    if at(STEP[name], 1, b + 1):
                        act.wait_ge(s_made[name], b + 2)
                        need(act, s_parts, (b + 1) * 2 * PARTS * 16)
                        nc.scalar.activation(dst[:, 0, :], MB[:, :], ACT.Copy, scale=SCALE if name == "q" else 1.0)\
                            .then_inc(s_part1, 1)
                if at(STEP["h2T"], 1, b - 2):
                    act.wait_ge(s_made["h2T"], b - 1)
                    need(act, s_made["l0_3"], b - 2)
                    nc.scalar.activation(h2T[:, :], MB[:, :], ACT.Identity, scale=col(3, b - 2), bias=col(2, b - 2))\
                        .then_inc(s_taken["h2T"], 1)
                if at(7, 1, b - 1):
                    for g in range(2):
                        act.wait_ge(s_gat[g], b * NQ * QUAD * 16)
                    nc.scalar.activation(den[:, :], den[:, :], ACT.Ln).then_inc(s_dln, 1)
                if at(8, 0, b - 1):
                    act.wait_ge(s_dln, b)
                    nc.scalar.activation(den[:, :], den[:, :], ACT.Exp, scale=-1.0).then_inc(s_dinv, 1)
                if at(9, 0, b + 2):
                    act.wait_ge(s_mv1, b + 3)
                    need(act, s_xn, b + 2)
                    nc.scalar.activation(rs1[:, :], mv1[:, :, 1], ACT.Ln, bias=epst[:, 0:1]).then_inc(s_ln1, 1)
                if at(9, 1, b + 2):
                    act.wait_ge(s_ln1, b + 3)
                    nc.scalar.activation(rs1[:, :], rs1[:, :], ACT.Exp, scale=-0.5).then_inc(s_rs1, 1)
                if at(13, 1, b - 1):
                    act.wait_ge(s_mv2, b)
                    need(act, s_x1n, b - 1)
                    nc.scalar.activation(rs2[:, :], mv2[:, :, 1], ACT.Ln, bias=epst[:, 0:1]).then_inc(s_ln2, 1)
                if at(14, 0, b - 1):
                    act.wait_ge(s_ln2, b)
                    nc.scalar.activation(rs2[:, :], rs2[:, :], ACT.Exp, scale=-0.5).then_inc(s_rs2, 1)

            for n in range(H):
                from_z(n, 0)
                log_of(n)
                misc(n, 0)
                from_z(n, 1)
                exp_of(n)
                misc(n, 1)

        @block.scalar
        def _(act):
            act_setup(act)
            batches(lambda b: act_batch(act, b))(nc.scalar)

        def dve_setup(dve):
            nc.vector.memset(epst[:, :], EPS).then_inc(s_eps, 1)
            dve.wait_ge(s_xa, 16)
            for t in range(TB):
                bn = nc.vector.bn_stats(st1[:, t, :], xa[:, t, :])
            bn.then_inc(s_st1, 1)
            dve.wait_ge(s_st1, 1)
            for t in range(TB):
                bn = nc.vector.bn_aggr(mv1[:, t, :], st1[:, t, :])
            bn.then_inc(s_mv1, 1)
            dve.wait_ge(s_cexp, 1)
            nc.vector.tensor_scalar(c_exp, c_exp, 1.0, None, ALU.add).then_inc(s_silu, 1)
            dve.wait_ge(s_silu, 1)
            nc.vector.reciprocal(c_inv, c_exp).then_inc(s_silu, 1)
            dve.wait_ge(s_silu, 2)
            nc.vector.tensor_tensor(c_sil, c_rows, c_inv, ALU.mult).then_inc(s_silu, 1)
            dve.wait_ge(s_rs1, 1)
            for t in range(TB):
                last = nc.vector.tensor_scalar(xn[:, t, :], xa[:, t, :], mv1[:, t, 0:1], rs1[:, t:t + 1],
                                               ALU.subtract, ALU.mult)
            last.then_inc(s_xn, 1)
            dve.wait_ge(s_csT, 1)
            nc.vector.tensor_copy(csil, MB[:, 0:B]).then_inc(s_csil, 1)
            dve.wait_ge(s_wT, 1)
            for i, w in enumerate((wq, wk)):
                nc.vector.tensor_copy(w[:, :].rearrange("p (g d j) -> p g d j", g=NQ, d=HD),
                                      SA[:, 0, i * D:(i + 1) * D].rearrange("p (g j d) -> p g d j", g=NQ, d=HD))
            nc.vector.tensor_copy(wv[:, :], SA[:, 0, 2 * D:3 * D])
            nc.vector.tensor_copy(wo[:, :], SA[:, 0, 3 * D:4 * D]).then_inc(s_wcp, 1)
            dve.wait_ge(s_modp, 1)
            M4 = MB[:, 64:64 + 4 * B].rearrange("p (i b) -> p i b", i=4)
            nc.vector.tensor_copy(mod[:, :, :], M4).then_inc(s_mod, 1)
            dve.wait_ge(s_mod, 1)
            for i in (1, 3):
                nc.vector.tensor_scalar(mod[:, i, :], mod[:, i, :], 1.0, None, ALU.add).then_inc(s_mod, 1)
            nc.vector.tensor_copy(g_in, SA[0:B, 1, 0:2 * D]).then_inc(s_gate, 1)

        def dve_gates(dve):
            dve.wait_ge(s_gate, 1)
            nc.vector.tensor_scalar(g_sign, g_in, 0.0, 2.0, ALU.is_ge, ALU.mult)
            nc.vector.tensor_scalar(g_abs, g_in, -1.0, None, ALU.mult).then_inc(s_gate, 1)
            dve.wait_ge(s_gate, 2)
            nc.vector.tensor_tensor(g_abs, g_abs, g_in, ALU.max).then_inc(s_gate, 1)
            dve.wait_ge(s_gate, 3)
            nc.vector.tensor_scalar(g_abs, g_abs, 0.25, None, ALU.max)
            nc.vector.tensor_scalar(g_sign, g_sign, -1.0, None, ALU.add).then_inc(s_gate, 1)
            dve.wait_ge(s_gate, 4)
            nc.vector.tensor_tensor(g_sign, g_sign, g_abs, ALU.mult).then_inc(s_gate, 1)
            dve.wait_ge(s_gate, 5)
            dve.wait_ge(ld_s, 4 * 16)
            nc.vector.tensor_scalar(g_row[:, 0:D], g_sign[:, 0:D], 1.0, None, ALU.mult)
            nc.vector.tensor_tensor(g_row[:, D:2 * D], g_sign[:, 0:D], bo8, ALU.mult)
            nc.vector.tensor_scalar(g_row[:, 2 * D:3 * D], g_sign[:, D:2 * D], sv[0:B, 2:3], None, ALU.mult)\
                .then_inc(s_gate, 1)
            nc.vector.tensor_scalar(sv[:, 0:2], sv[:, 0:2], 2.0, None, ALU.mult).then_inc(s_sv, 1)
            nc.vector.memset(OP[:, :], 0.0)
            dve.wait_ge(s_sv, 1)
            dve.wait_ge(ld_k, 3 * 16)
            nc.vector.tensor_tensor(W0[:, :], k0u[:, 0, :], k0u[:, 1, :], ALU.subtract).then_inc(s_W0, 1)
            dve.wait_ge(s_W0, 1)
            nc.vector.tensor_scalar(W0[:, :], W0[:, :], 2.0, None, ALU.mult).then_inc(s_W0, 1)

        def dve_batch(dve, b):
            def from_z(n, h):
                if not live(b) or PATHS[n][h] == "A":
                    return
                if PATHS[n][h] == "D":
                    i = before("D", n, h)
                    need(dve, s_sq, b * N_D + i)
                    need(dve, s_p, H * b + n + 1 - F_RING)
                    nc.vector.scalar_tensor_tensor(cub[:, n % F_RING, h, :], sq[:, (i - 1) % 2, :], 3.0, Z[:, h, :],
                                                   ALU.add, ALU.mult).then_inc(s_cv, 1)
                else:
                    i = before("AV", n, h)
                    need(dve, s_z, 2 * H * b + 2 * n + h + 1)
                    need(dve, s_cp, b * N_P + i - 2)
                    nc.vector.tensor_copy(zc[:, (i - 1) % 2, :], Z[:, h, :]).then_inc(s_zv, 1)

            def maxima(n, qts):
                beta, g = (b, n // QUAD + 2) if n < 8 else (b + 1, n // QUAD - 2)
                if not live(beta):
                    return
                j = n % QUAD
                for qt in qts:
                    need(dve, s_a, 64 * beta + TB * (QUAD * g + j) + qt + 1)
                    if j == 0 and qt == 0:
                        need(dve, s_mt, NQ * beta + g - 1)
                    nc.vector.tensor_reduce(mx[:, g % 2, j * TB + qt:j * TB + qt + 1], SA[:, qt % 2, :], AX_X, ALU.max)\
                        .then_inc(s_mx, 1)

            def take_maxima(n):
                beta, g = quad_before(b, n)
                if n % QUAD or not live(beta):
                    return
                i = NQ * beta + g
                dve.wait_ge(s_mt, i + 1)
                need(dve, s_mp, 4 * i)
                nc.vector.tensor_scalar(ms[:, :], SA[0:QUAD * TB, 1, 0:P], -1.0, -1.0, ALU.mult, ALU.add)\
                    .then_inc(s_ms, 1)

            def relu_of(name, beta):
                layer, m = int(name[1]), int(name[3])
                dve.wait_ge(s_made[name], beta + 1)
                last = "l1_3" if layer == 0 else "y"
                if m == 0:
                    need(dve, s_made[last], beta)
                nc.vector.tensor_scalar(hid[layer][:, m, :], MB[:, :], sv[:, layer:layer + 1], 0.0, ALU.mult, ALU.max)\
                    .then_inc(s_taken[name], 1)

            def misc(n, place):
                def at(step, where, beta):
                    return (n, place) == (step, where) and live(beta)

                for i, (step, name, src, scale) in enumerate(((STEP["q"], "q", SQ, SCALE), (STEP["k"], "k", SK, 1.0))):
                    if at(step, 1, b + 1):
                        dve.wait_ge(s_part1, 2 * (b + 1) + i + 1)
                        need(dve, s_part3, 2 * b + i + 1)
                        nc.vector.scalar_tensor_tensor(rem[:, i, :], MB[:, :], scale, src[:, 0, :],
                                                       ALU.mult, ALU.subtract).then_inc(s_taken[name], 1)
                for step, name, _ in MISC:
                    if name[:2] in ("l0", "l1") and at(step, 1, b - 2):
                        relu_of(name, b - 2)
                if n % QUAD == (LAG + QUAD - 1) % QUAD and place == 1:
                    q = (n - LAG) // QUAD - 1
                    beta, g = (b, q) if q >= 0 else (b - 1, q + NQ)
                    if live(beta):
                        i = NQ * beta + g
                        dve.wait_ge(s_pv, QUAD * (i + 1))
                        need(dve, s_gat[g % 2], (2 * beta + g // 2) * 2 * QUAD * 16)
                        nc.vector.tensor_copy(OT[:, g % 2, :], OP[:, :]).then_inc(s_ot, 1)
                if at(6, 0, b + 2):
                    dve.wait_ge(s_xa, 16 * (b + 3))
                    for t in range(TB):
                        bn = nc.vector.bn_stats(st1[:, t, :], xa[:, t, :])
                    bn.then_inc(s_st1, 1)
                if at(7, 1, b + 2):
                    dve.wait_ge(s_st1, b + 3)
                    need(dve, s_xn, b + 2)
                    apart(dve, b)
                    for t in range(TB):
                        bn = nc.vector.bn_aggr(mv1[:, t, :], st1[:, t, :])
                    bn.then_inc(s_mv1, 1)
                if at(STEP["x1"], 1, b - 1):
                    dve.wait_ge(s_made["x1"], b)
                    dve.wait_ge(s_xb, 16 * b)
                    need(dve, s_x1k, b - 1)
                    need(dve, s_x1n, b - 1)
                    nc.vector.tensor_tensor(x1[:, :, :], MB4, xb[:, :, :], ALU.add).then_inc(s_taken["x1"], 1)
                if at(11, 0, b - 1):
                    dve.wait_ge(s_taken["x1"], b)
                    for t in range(TB):
                        bn = nc.vector.bn_stats(st2[:, t, :], x1[:, t, :])
                    bn.then_inc(s_st2, 1)
                if at(12, 0, b - 1):
                    dve.wait_ge(s_st2, b)
                    need(dve, s_x1n, b - 1)
                    apart(dve, b)
                    for t in range(TB):
                        bn = nc.vector.bn_aggr(mv2[:, t, :], st2[:, t, :])
                    bn.then_inc(s_mv2, 1)
                if at(STEP["v"], 1, b + 1):
                    dve.wait_ge(s_made["v"], b + 2)
                    need(dve, s_vq, NQ * (b + 1))
                    nc.vector.tensor_copy(Vn[:, :, :, :].rearrange("p t h d -> p t (h d)"), MB4)\
                        .then_inc(s_taken["v"], 1)
                if at(STEP["y"], 1, b - 2):
                    dve.wait_ge(s_made["y"], b - 1)
                    need(dve, s_x1k, b - 1)
                    need(dve, s_out, 16 * (b - 2))
                    nc.vector.tensor_tensor(y[:, :, :], MB4, x1k[:, :, :], ALU.add).then_inc(s_taken["y"], 1)

            for n in range(H):
                from_z(n, 0)
                maxima(n, (0, 1))
                misc(n, 0)
                from_z(n, 1)
                take_maxima(n)
                maxima(n, (2, 3))
                misc(n, 1)
                if n == 5 and isinstance(b, int) and b == -1:
                    dve_gates(dve)

        @block.vector
        def _(dve):
            dve_setup(dve)
            batches(lambda b: dve_batch(dve, b))(nc.vector)

        def pool_setup(pool):
            nc.gpsimd.memset(ident[:, :], 0.0).then_inc(s_id, 1)
            pool.wait_ge(s_id, 1)
            nc.gpsimd.affine_select(out=ident[:, :], in_=ident[:, :], compare_op=ALU.not_equal, fill=1.0, base=0,
                                    pattern=[[-1, P]], channel_multiplier=1).then_inc(s_id, 1)
            for t in (QH, KH):
                nc.gpsimd.memset(t[:, :, :].bitcast(F32), 0.0).then_inc(s_one, 1)
            pool.wait_ge(s_one, 2)
            nc.gpsimd.memset(KH[MROW:MROW + PARTS, :, :], 1.0).then_inc(s_one, 1)
            pool.wait_ge(s_one, 3)
            nc.gpsimd.memset(Vq[:, :, :, HD:2 * HD], 1.0).then_inc(s_one, 1)
            nc.gpsimd.memset(one[:, :], 1.0).then_inc(s_one, 1)
            pool.wait_ge(ld_k, 3 * 16)
            nc.gpsimd.tensor_scalar(W1[:, :, :], k1u, 2.0, -1.0, ALU.mult, ALU.add).then_inc(s_wts, 1)
            nc.gpsimd.tensor_scalar(W2[:, :, :], k2u, 2.0, -1.0, ALU.mult, ALU.add).then_inc(s_wts, 1)

        def pool_batch(pool, b):
            def from_z(n, h):
                if not live(b) or PATHS[n][h] == "D":
                    return
                i = before("AV", n, h)
                if PATHS[n][h] == "A":
                    need(pool, s_za, b * N_A + before("A", n, h))
                else:
                    need(pool, s_zv, b * N_V + before("V", n, h))
                need(pool, s_p, H * b + n + 1 - F_RING)
                zz, cc = zc[:, (i - 1) % 2, :], cub[:, n % F_RING, h, :]
                nc.gpsimd.tensor_tensor(cc, zz, zz, ALU.mult).then_inc(s_q1, 1)
                need(pool, s_q1, 2 * (b * N_P + i) - 1)
                apart(pool, b)
                nc.gpsimd.tensor_scalar(cc, cc, 1.0, 3.0, ALU.mult, ALU.add).then_inc(s_q1, 1)
                need(pool, s_q1, 2 * (b * N_P + i))
                nc.gpsimd.tensor_tensor(cc, cc, zz, ALU.mult).then_inc(s_cp, 1)

            def normalise(beta, src, mv, rs, dst, s_rs, s_free, s_done, free):
                pool.wait_ge(s_rs, beta + 1)
                need(pool, s_free, free)
                apart(pool, beta)
                for t in range(TB):
                    last = nc.gpsimd.tensor_scalar(dst[:, t, :], src[:, t, :], mv[:, t, 0:1], rs[:, t:t + 1],
                                                   ALU.subtract, ALU.mult)
                last.then_inc(s_done, 1)

            def v_in(beta, g):
                if live(beta):
                    i = NQ * beta + g
                    pool.wait_ge(s_taken["v"], beta + 1)
                    need(pool, s_pv, QUAD * (i + 1 - NQ))
                    apart(pool, beta)
                    hs = slice(QUAD * g, QUAD * (g + 1))
                    nc.gpsimd.tensor_copy(Vq[:, :, hs, 0:HD], Vn[:, :, hs, :]).then_inc(s_vq, 1)

            def misc(n, place):
                def at(step, where, beta):
                    return (n, place) == (step, where) and live(beta)

                for i, (name, dst) in enumerate((("q", SQ), ("k", SK))):
                    if at(STEP[name] + 1, 0, b + 1):
                        k = 2 * (b + 1) + i + 1
                        pool.wait_ge(s_taken["qk"[i]], b + 2)
                        apart(pool, b)
                        nc.gpsimd.tensor_scalar(dst[:, 1, :], rem[:, i, :], 1.0, 0.0, ALU.mult, ALU.add)\
                            .then_inc(s_part2, 1)
                        pool.wait_ge(s_part2, k)
                        nc.gpsimd.tensor_tensor(dst[:, 2, :], rem[:, i, :], dst[:, 1, :], ALU.subtract)\
                            .then_inc(s_part3, 1)
                if n % QUAD == 1 and place == 0:
                    beta, gg = quad_before(b, n - 1)
                    if live(beta):
                        k = 4 * (NQ * beta + gg)
                        pool.wait_ge(s_ms, NQ * beta + gg + 1)
                        need(pool, s_mrow[(gg - 1) % NQ], (beta + (gg > 0)) * PARTS * 16)
                        apart(pool, b)
                        nc.gpsimd.tensor_scalar(mp[:, 0, :], ms[:, :], 1.0, 0.0, ALU.mult, ALU.add).then_inc(s_mp, 1)
                        pool.wait_ge(s_mp, k + 1)
                        nc.gpsimd.tensor_tensor(mrem[:, :], ms[:, :], mp[:, 0, :], ALU.subtract)\
                            .then_inc(s_mp, 1)
                        pool.wait_ge(s_mp, k + 2)
                        apart(pool, b)
                        nc.gpsimd.tensor_scalar(mp[:, 1, :], mrem[:, :], 1.0, 0.0, ALU.mult, ALU.add).then_inc(s_mp, 1)
                        pool.wait_ge(s_mp, k + 3)
                        nc.gpsimd.tensor_tensor(mp[:, 2, :], mrem[:, :], mp[:, 1, :], ALU.subtract)\
                            .then_inc(s_mp, 1)
                if at(8, 1, b - 1):
                    pool.wait_ge(s_dinv, b)
                    nc.gpsimd.tensor_tensor(num[:, :], num[:, :], den[:, :], ALU.mult)\
                        .then_inc(s_att, 1)
                if at(5, 1, b - 2):
                    pool.wait_ge(s_gB, 16 * (b - 1))
                    need(pool, s_made["y"], b - 2)
                    for kc in range(KC):
                        tt = nc.gpsimd.tensor_tensor(W2G[:, kc, :], W2[:, kc, :], gB[:, :], ALU.mult)
                    tt.then_inc(s_w2g, 1)
                if at(6, 1, b - 1):
                    pool.wait_ge(s_gA, 16 * b)
                    need(pool, s_made["x1"], b - 1)
                    nc.gpsimd.tensor_tensor(woG[:, :], wo[:, :], gA[:, 0:D], ALU.mult).then_inc(s_wog, 1)
                if at(10, 1, b + 2):
                    normalise(b + 2, xa, mv1, rs1, xn, s_rs1, s_made["hT"], s_xn, b + 2)
                if at(0, 0, b - 2) :
                    pool.wait_ge(s_taken["x1"], b - 1)
                    need(pool, s_taken["y"], b - 2)
                    apart(pool, b)
                    nc.gpsimd.tensor_scalar(x1k[:, :, :], x1[:, :, :], 1.0, 0.0, ALU.mult, ALU.add).then_inc(s_x1k, 1)
                if at(14, 1, b - 1):
                    normalise(b - 1, x1, mv2, rs2, x1n, s_rs2, s_made["h2T"], s_x1n, b - 1)
                if (n, place) == (3, 1):
                    v_in(b, 2)
                if (n, place) == (6, 0):
                    v_in(b, 3)
                if (n, place) == (15, 1):
                    v_in(b + 1, 0)
                    v_in(b + 1, 1)

            for n in range(H):
                from_z(n, 0)
                misc(n, 0)
                from_z(n, 1)
                misc(n, 1)

        @block.gpsimd
        def _(pool):
            pool_setup(pool)
            batches(lambda b: pool_batch(pool, b))(nc.gpsimd)

        def sp_setup(sp):
            sp.dma_start(xa[:, :, :], x_t[:, 0:TB, :]).then_inc(s_xa, 16)
            sp.dma_start(c_rows, c).then_inc(ld_c, 16)
            sp.dma_start(w_rows[:, 0:3, :], w_qkv.rearrange("(k p) d -> p k d", p=P)).then_inc(ld_w, 16)
            sp.dma_start(wm, wmod).then_inc(ld_w, 16)
            sp.dma_start(w_rows[:, 3, :], w_out).then_inc(ld_w, 16)
            for i, s in enumerate((s0, s1, s2)):
                sp.dma_start(sv[:, i:i + 1], s.partition_broadcast(P)).then_inc(ld_s, 16)
            sp.dma_start(bo8, b_out.partition_broadcast(B)).then_inc(ld_s, 16)
            sp.dma_start(k0u, k0.rearrange("(a p) n -> p a n", p=P)).then_inc(ld_k, 16)
            sp.dma_start(k1u, k1.rearrange("(a p) n -> p a n", p=P)).then_inc(ld_k, 16)
            sp.dma_start(k2u, k2.rearrange("(a p) n -> p a n", p=P)).then_inc(ld_k, 16)

        def sp_need(sp, b, s, n):
            need(sp, s, n)
            apart(sp, b)

        def sp_batch(sp, b):
            for g in range(NQ):
                if g == 1 and live(b + 1):
                    sp_need(sp, b, s_qk[NQ - 1], (b + 1) * E_DMAS * 16)
                    for i, (src, dst) in enumerate(((SQ, parts_q), (SK, parts_k))):
                        for a in range(PARTS):
                            if a < 2:
                                sp_need(sp, b, s_part3 if a else s_part1, 2 * (b + 1) + i + 1)
                            sp.dma_start(dst[:, a], src[:, a, :]).then_inc(s_parts, 16)
                beta, gg = (b, NQ - 1) if g == 0 else (b + 1, g - 1)
                if live(beta):
                    if g == 1:
                        sp_need(sp, b, s_parts, (beta + 1) * 2 * PARTS * 16)
                    sp_need(sp, b, s_z, 2 * QUAD * (NQ * (beta - 1) + gg + 1))
                    if isinstance(beta, int) and beta == 0 and gg == 0:
                        sp.wait_ge(s_one, 3)
                    heads = slice(QUAD * gg, QUAD * gg + QUAD)
                    for a in range(PARTS):
                        r = a * PARTS * HD
                        rows = parts_q[gg, a].rearrange("(d j) s -> d (j s)", d=HD)
                        sp.dma_start(QH[r:r + PARTS * HD, heads, :], rows.partition_broadcast(PARTS)).then_inc(s_qk[gg], 16)
                    rows = parts_k[gg].rearrange("c (d j) s -> (c d) (j s)", d=HD)
                    sp.dma_start(KH[0:NROW, heads, :], rows.partition_broadcast(PARTS)).then_inc(s_qk[gg], 16)
                if g == 2 and isinstance(b, int) and b == -1:
                    sp.wait_ge(s_gate, 6)
                    sp.dma_start(gate_rows, g_row).then_inc(s_gw, 16)
                if g == 0 and live(b + 2):
                    sp_need(sp, b, s_xn, b + 2)
                    sp.dma_start(xa[:, :, :], x_t[:, bass.ds((b + 2) * TB, TB), :]).then_inc(s_xa, 16)
                beta, gg = (b, g + 1) if g < NQ - 1 else (b + 1, 0)
                if live(beta):
                    sp_need(sp, b, s_mp, 4 * (NQ * beta + gg + 1))
                    for a in range(PARTS):
                        sp.dma_start(QH[MROW + a:MROW + a + 1, QUAD * gg:QUAD * gg + QUAD, :], mp[:, a, :])\
                            .then_inc(s_mrow[gg], 16)
                if g == 1 and live(b - 1):
                    if isinstance(b, int) and b == 1:
                        sp.wait_ge(s_gw, 16)
                    sp_need(sp, b, s_made["x1"], b - 1)
                    sp.dma_start(gA[:, :], gate_rows[bass.ds(b - 1, 1), 0:2 * D].partition_broadcast(P)).then_inc(s_gA, 16)
                if g == 1 and live(b - 2):
                    sp_need(sp, b, s_w2g, b - 2)
                    sp.dma_start(gB[:, :], gate_rows[bass.ds(b - 2, 1), 2 * D:3 * D].partition_broadcast(P)).then_inc(s_gB, 16)
                if g == 2 and live(b - 1):
                    sp_need(sp, b, s_taken["x1"], b - 1)
                    sp.dma_start(xb[:, :, :], x_t[:, bass.ds((b - 1) * TB, TB), :]).then_inc(s_xb, 16)
                beta, gg = (b, g - 2) if g >= 2 else (b - 1, g + 2)
                if live(beta):
                    sp_need(sp, b, s_ot, NQ * beta + gg + 1)
                    if gg == 0:
                        sp_need(sp, b, s_made["x1"], beta)
                    for j in range(QUAD):
                        r = 32 * gg + HD * j
                        sp.dma_start(num[r:r + HD, :], OT[32 * j:32 * j + HD, gg % 2, :]).then_inc(s_gat[gg % 2], 16)
                        sp.dma_start(den[r:r + HD, :], OT[32 * j + HD:32 * j + 2 * HD, gg % 2, :]).then_inc(s_gat[gg % 2], 16)
                if g == 3 and live(b - 2):
                    sp_need(sp, b, s_taken["y"], b - 1)
                    sp.dma_start(out_t[:, bass.ds((b - 2) * TB, TB), :], y[:, :, :]).then_inc(s_out, 16)

        @block.sync
        def _(sp):
            sp_setup(sp)
            batches(lambda b: sp_batch(sp, b))(nc.sync)
            sp.wait_ge(s_out, 16 * B)


_INS = ["L0_attn_x", "L0_attn_w_qkv", "L0_attn_w_out", "L0_attn_b_out", "L0_ffn_k0", "L0_ffn_k1", "L0_ffn_k2",
        "L0_ffn_s0", "L0_ffn_s1", "L0_ffn_s2", "L0_c", "L0_wmod"]


def kernel(**inputs):
    import numpy as np
    import concourse.bacc as bacc
    from concourse.bass_utils import run_bass_kernel_spmd

    nc = bacc.Bacc("TRN2", target_bir_lowering=False, num_devices=1)
    arrays, args = {}, []
    for name in _INS:
        a = np.ascontiguousarray(inputs[name])
        if a.ndim == 0:
            a = a.reshape(1)
        arrays[name] = a
        args.append(nc.dram_tensor(name, a.shape, mybir.dt.from_np(a.dtype), kind="ExternalInput").ap())
    out = nc.dram_tensor("out", (B, S, D), F32, kind="ExternalOutput").ap()
    adaln_block(nc, *args, out)
    r = run_bass_kernel_spmd(nc, [arrays], core_ids=[0])
    return r.results[0]["out"]
```

```python
from contextlib import ExitStack

import numpy as np
import concourse.bass as bass
from concourse import mybir

F32 = mybir.dt.float32
BF16 = mybir.dt.bfloat16
U8 = mybir.dt.uint8
ALU = mybir.AluOpType
ACT = mybir.ActivationFunctionType
AX_X = mybir.AxisListType.X

P = 128
B = 8
S = 512
D = 128
H = 16
HD = D // H
QUAD = 4
NQ = H // QUAD
TB = S // P
HALF = 2 * S
F = 512
KC = F // P
PARTS = 3
NROW = PARTS * PARTS * HD
MROW = 96
EPS = 1e-5
TWO_ONES = float(np.array([0x3F803F80], np.uint32).view(np.float32)[0])
E_DMAS = PARTS + 1
SCALE = HD ** -0.5
FIRST = -1


PATHS = "VVDDVVAAVAVDVAAD"
P_RING = 8
F_RING = 2

LAG = 2


def before(kinds, n):
    return sum(PATHS[m] in kinds for m in range(n + 1))


N_A = before("A", H - 1)
N_V = before("V", H - 1)
N_P = N_A + N_V
assert N_P % 2 == 0

CHUNKS = 4
assert CHUNKS == KC == TB


def short(name, off, step, place=0, point="e"):
    return name, off, [(step, place, CHUNKS)], (step, point)


def long_(name, off, step):
    return name, off, [(step, 0, CHUNKS // 2), (step, 1, CHUNKS // 2)], (step + 1, "s")


MISC = [
    short("hT", 1, 0), short("q", 1, 1), short("k", 1, 2), short("h2T", -2, 3),
    short("l0_0", -2, 4), short("l0_1", -2, 5), short("l0_2", -2, 6), short("l0_3", -2, 7), short("v", 1, 8),
    long_("l1_0", -2, 9), long_("l1_1", -2, 10), long_("l1_2", -2, 11), short("x1", -1, 12), long_("l1_3", -2, 13),
    ("y", -2, [(14, 0, 2), (14, 1, 1), (15, 0, 1)], (15, "e")),
]
MISC_LAST = {
    B - 1: [short("h2T", -2, 0), *(short(f"l0_{m}", -2, m + 1) for m in range(KC)),
            *(long_(f"l1_{m}", -2, m + 5) for m in range(KC)), short("x1", -1, 9), long_("y", -2, 9),
            short("h2T", -1, 12), short("l0_0", -1, 13), short("l0_1", -1, 13), short("l0_2", -1, 14),
            short("l0_3", -1, 14), long_("l1_0", -1, 15)],
    B: [long_("l1_1", -2, 0), long_("l1_2", -2, 6), long_("l1_3", -2, 7), short("x1", -1, 8), long_("y", -2, 9),
        short("h2T", -1, 10)],
    B + 1: [*(short(f"l0_{m}", -2, m) for m in range(KC)), *(long_(f"l1_{m}", -2, m + 4) for m in range(KC)),
            long_("y", -2, 8)],
}
EVENTS = {
    "den_ln": (7, 1), "den_exp": (8, 0), "att": (8, 1, "pool"), "st2": (13, 0), "mv2": (14, 0), "rs2_ln": (14, 1),
    "rs2_exp": (15, 0), "x1n": (15, 0, "pool"), "w2g": (11, 1), "wog": (5, 1), "xbg": (7, 1),
}
EVENTS_LAST = {
    B - 1: {"st2": (10, 0), "mv2": (10, 1), "rs2_ln": (11, 0), "rs2_exp": (11, 0), "x1n": (11, 1, "dve"), "w2g": (6, 1)},
    B: {"den_ln": (7, 0), "den_exp": (7, 1), "att": (8, 0, "dve"), "st2": (8, 1), "mv2": (9, 0), "rs2_ln": (9, 0),
        "rs2_exp": (9, 0), "x1n": (9, 0, "dve"), "w2g": (6, 1)},
    B + 1: {"w2g": (5, 1)},
}


def is_first(b):
    return isinstance(b, int) and b == FIRST


def misc_of(b):
    return MISC_LAST.get(b, MISC) if isinstance(b, int) else MISC


def event(b, name):
    return EVENTS_LAST.get(b, {}).get(name, EVENTS[name]) if isinstance(b, int) else EVENTS[name]


def live(beta):
    return not isinstance(beta, int) or 0 <= beta < B


def adaln_block(nc, x, w_qkv, w_out, b_out, k0, k1, k2, s0, s1, s2, c, wmod, out):
    x_t = x.rearrange("b (t p) d -> p (b t) d", p=P)
    parts_q = nc.dram_tensor("parts_q", (NQ, PARTS, QUAD * HD, S), BF16, kind="Internal").ap()
    parts_k = nc.dram_tensor("parts_k", (NQ, PARTS, QUAD * HD, S), BF16, kind="Internal").ap()
    gate_rows = nc.dram_tensor("gate_rows", (B, 3 * D), F32, kind="Internal").ap()
    out_t = out.rearrange("b (t p) d -> p (b t) d", p=P)

    with ExitStack() as ctx:
        def sb(name, shape, dt=F32):
            return ctx.enter_context(nc.sbuf_tensor(name, shape, dt))

        def sem(name):
            return ctx.enter_context(nc.semaphore(name))

        Z = ctx.enter_context(nc.psum_tensor("Z", [P, 2, HALF], F32))
        SA = ctx.enter_context(nc.psum_tensor("SA", [P, 2, S], F32))
        OP = ctx.enter_context(nc.psum_tensor("OP", [P, S], F32))
        MB = ctx.enter_context(nc.psum_tensor("MB", [P, S], F32))

        QH = sb("QH", [P, H, S], BF16)
        KH = sb("KH", [P, H, S], BF16)
        prob = sb("prob", [P, P_RING, TB * S])
        cub = sb("cub", [P, F_RING, 2, HALF])
        sq = sb("sq", [P, 2, HALF])
        zc = sb("zc", [P, 2, S])
        Vq = sb("Vq", [P, TB, H, HD, 2])
        Vn = sb("Vn", [P, TB, H, HD])
        SQ = sb("SQ", [P, PARTS, S], BF16)
        SK = sb("SK", [P, PARTS, S], BF16)
        rem = sb("rem", [P, 2, S])
        mx = sb("mx", [P, 2, QUAD * TB])
        ms = sb("ms", [QUAD * TB, P])
        mrem = sb("mrem", [QUAD * TB, P])
        mp = sb("mp", [QUAD * TB, PARTS, P], BF16)
        OT = sb("OT", [P, 2, S])
        nd = sb("nd", [P, 2, S])
        num, den = nd[:, 0, :], nd[:, 1, :]
        xa = sb("xa", [P, TB, D])
        xn = sb("xn", [P, TB, D])
        hT = sb("hT", [P, S])
        xb = sb("xb", [P, TB, D])
        woG = sb("woG", [P, D])
        W2G = sb("W2G", [P, KC, D])
        gA = sb("gA", [P, 2 * D])
        gB = sb("gB", [P, D])
        x1 = sb("x1", [P, TB, D])
        x1k = sb("x1k", [P, TB, D])
        x1n = sb("x1n", [P, TB, D])
        h2T = sb("h2T", [P, S])
        hid = [sb("hid0", [P, KC, S]), sb("hid1", [P, KC, S])]
        y = sb("y", [P, TB, D])
        wq = sb("wq", [P, D])
        wk = sb("wk", [P, D])
        wv = sb("wv", [P, D])
        wo = sb("wo", [P, D])
        W0 = sb("W0", [P, F])
        W1 = sb("W1", [P, KC, F])
        W2 = sb("W2", [P, KC, D])
        ident = sb("ident", [P, P])
        mod = sb("mod", [P, 4, B])
        sv = sb("sv", [P, 3])
        st1 = sb("st1", [P, TB, 6])
        mv1 = sb("mv1", [P, TB, 2])
        rs1 = sb("rs1", [P, TB])
        st2 = sb("st2", [P, TB, 6])
        mv2 = sb("mv2", [P, TB, 2])
        rs2 = sb("rs2", [P, TB])
        epst = sb("epst", [P, 1])

        stage = prob[:, 0, :]
        w_rows = stage[:, 0:4 * D].rearrange("p (k d) -> p k d", k=4)
        wm = stage[:, 512:512 + 6 * D]
        csil = stage[:, 1296:1296 + B]
        c_rows = stage[0:B, 1408:1408 + D]
        c_exp = stage[0:B, 1536:1536 + D]
        c_inv = stage[0:B, 1664:1664 + D]
        c_sil = stage[0:B, 1792:1792 + D]
        side = prob[0:B, 2, :]
        g_in = side[:, 0:2 * D]
        g_sign = side[:, 256:256 + 2 * D]
        g_abs = side[:, 512:512 + 2 * D]
        g_row = side[:, 768:768 + 3 * D]
        bo8 = side[:, 1280:1280 + D]
        k_u8 = prob[:, 1, :].bitcast(U8)
        k0u = k_u8[:, 0:2 * F].rearrange("p (a n) -> p a n", a=2)
        k1u = k_u8[:, 1024:1024 + KC * F].rearrange("p (a n) -> p a n", a=KC)
        k2u = k_u8[:, 4096:4096 + KC * D].rearrange("p (a n) -> p a n", a=KC)

        ld_c = sem("ld_c")
        ld_w = sem("ld_w")
        ld_s = sem("ld_s")
        ld_k = sem("ld_k")
        s_id = sem("s_id")
        s_apart = sem("s_apart")
        s_eps = sem("s_eps")
        s_cexp = sem("s_cexp")
        s_silu = sem("s_silu")
        s_csT = sem("s_csT")
        s_csil = sem("s_csil")
        s_wT = sem("s_wT")
        s_wcp = sem("s_wcp")
        s_modp = sem("s_modp")
        s_gatep = sem("s_gatep")
        s_mod = sem("s_mod")
        s_gate = sem("s_gate")
        s_gw = sem("s_gw")
        s_sv = sem("s_sv")
        s_wts = sem("s_wts")
        s_W0 = sem("s_W0")
        s_gA = sem("s_gA")
        s_gB = sem("s_gB")
        s_xbg = sem("s_xbg")
        s_wog = sem("s_wog")
        s_w2g = sem("s_w2g")
        s_parts = {n: sem("s_parts_" + n) for n in "qk"}
        s_z = sem("s_z")
        s_sq = sem("s_sq")
        s_za = sem("s_za")
        s_zv = sem("s_zv")
        s_cv = sem("s_cv")
        s_q1 = sem("s_q1")
        s_cp = sem("s_cp")
        s_ln = sem("s_ln")
        s_p = sem("s_p")
        s_pv = sem("s_pv")
        s_a = sem("s_a")
        s_mx = sem("s_mx")
        s_mt = sem("s_mt")
        s_ms = sem("s_ms")
        s_mp = sem("s_mp")
        s_mrow = [sem(f"s_mrow{g}") for g in range(NQ)]
        s_qk = [sem(f"s_qk{g}") for g in range(NQ)]
        s_ot = sem("s_ot")
        s_gat = [sem(f"s_gat{g}") for g in range(2)]
        s_vq = sem("s_vq")
        s_one = sem("s_one")
        s_made = {m[0]: sem("made_" + m[0]) for m in MISC}
        s_taken = {m[0]: sem("taken_" + m[0]) for m in MISC}
        s_part1 = sem("s_part1")
        s_rem = sem("s_rem")
        s_part2 = sem("s_part2")
        s_part3 = sem("s_part3")
        s_xa = sem("s_xa")
        s_xb = sem("s_xb")
        s_st1 = sem("s_st1")
        s_mv1 = sem("s_mv1")
        s_ln1 = sem("s_ln1")
        s_rs1 = sem("s_rs1")
        s_xn = sem("s_xn")
        s_st2 = sem("s_st2")
        s_mv2 = sem("s_mv2")
        s_ln2 = sem("s_ln2")
        s_rs2 = sem("s_rs2")
        s_x1n = sem("s_x1n")
        s_x1k = sem("s_x1k")
        s_dln = sem("s_dln")
        s_dinv = sem("s_dinv")
        s_att = sem("s_att")
        s_out = sem("s_out")

        def need(eng, s, n):
            if not isinstance(n, int) or n > 0:
                eng.wait_ge(s, n)

        def apart(eng, b):
            if not isinstance(b, int):
                eng.sem_inc(s_apart)

        def z_taken(eng, b, n, h):
            need(eng, s_cv, 2 * H * b + 2 * n + h + 1)
            if h == 0 and PATHS[n] == "A":
                need(eng, s_za, b * N_A + before("A", n))
            if h == 0 and PATHS[n] == "V":
                need(eng, s_zv, b * N_V + before("V", n))

        def cubic_ready(eng, b, n, h):
            need(eng, s_cv, 2 * H * b + 2 * n + h + 1)
            if h == 0 and PATHS[n] != "D":
                need(eng, s_cp, b * N_P + before("AV", n))

        def of_vector(n, h):
            return slice(S if h == 0 and PATHS[n] != "D" else 0, HALF)

        def quad_before(b, n):
            return (b, n // QUAD + 1) if n // QUAD < NQ - 1 else (b + 1, 0)

        tail = [(b, i) for b in (B - 1, B, B + 1) for i, m in enumerate(misc_of(b))
                if b > B - 1 or m[2][0][0] > 8]
        BANKS = 3

        def bank_of(b, i):
            if is_first(b) and misc_of(b)[i][0] == "k":
                return SA[:, 0, :], None
            if not isinstance(b, int) or (b, i) not in tail:
                return MB[:, :], None
            k = tail.index((b, i))
            return (SA[:, k % BANKS - 1, :] if k % BANKS else MB[:, :]), k

        def products_at(b, n, points):
            return [(name, b + off, bank_of(b, i)[0]) for i, (name, off, _, (step, point)) in enumerate(misc_of(b))
                    if step == n and point in points and live(b + off)]

        def logits_bank(b, beta, h, qt):
            pair = (TB * h + qt) // 2
            if is_first(b) and pair % 3:
                return Z[:, pair % 3 - 1, :].rearrange("p (t s) -> p t s", t=2)
            return SA

        def batches(body):
            def run(eng):
                for b in range(FIRST, 3):
                    body(b)
                with eng.Fori(3, B - 2) as b:
                    body(b)
                for b in range(B - 2, B + 2):
                    body(b)
            return run

        def col(i, b):
            return mod[:, i, bass.ds(b, 1)]

        block = ctx.enter_context(nc.Block())

        def pe_setup(pe):
            pe.wait_ge(s_id, 2)
            pe.wait_ge(s_silu, 3)
            nc.tensor.transpose(MB[:, 0:B], c_sil, ident[0:B, 0:B]).then_inc(s_csT, 1)
            pe.wait_ge(ld_w, 3 * 16)
            for i in range(4):
                mm = nc.tensor.transpose(SA[:, 0, i * D:(i + 1) * D], w_rows[:, i, :], ident[:, :])
            mm.then_inc(s_wT, 1)
            pe.wait_ge(s_csil, 1)
            for n, i in enumerate((0, 1, 3, 4)):
                mm = nc.tensor.matmul(MB[:, 64 + n * B:64 + (n + 1) * B], wm[:, i * D:(i + 1) * D], csil,
                                 start=True, stop=True)
            mm.then_inc(s_modp, 1)
            for n, i in enumerate((2, 5)):
                mm = nc.tensor.matmul(SA[0:B, 1, n * D:(n + 1) * D], csil, wm[:, i * D:(i + 1) * D],
                                      start=True, stop=True)
            mm.then_inc(s_gatep, 1)
            pe.wait_ge(s_mod, 1)
            pe.wait_ge(s_wcp, 1)

        def misc_prev(b, i):
            while True:
                i, b = (i - 1, b) if i else (len(misc_of(b - 1)) - 1, b - 1)
                name, off = misc_of(b)[i][:2]
                if live(b + off):
                    return name, b + off
                if isinstance(b, int) and b < -2:
                    return None

        def misc_product(pe, b, i, chunks):
            name, off = misc_of(b)[i][:2]
            first, last = chunks[0] == 0, chunks[-1] == CHUNKS - 1
            beta = b + off
            if not live(beta):
                return
            if first:
                k = bank_of(b, i)[1]
                if is_first(b) and name == "k":
                    prev = None
                elif k is None or k == 0:
                    prev = misc_prev(b, i)
                elif k < BANKS:
                    pe.wait_ge(s_ms, NQ * B)
                    prev = None
                else:
                    pb, pi = tail[k - BANKS]
                    prev = misc_of(pb)[pi][0], pb + misc_of(pb)[pi][1]
                if prev:
                    need(pe, s_taken[prev[0]], prev[1] + 1)
            bank = bank_of(b, i)[0]
            bank4 = bank.rearrange("p (t d) -> p t d", t=TB)
            if name == "hT":
                pe.wait_ge(s_xn, beta + 1)
                for t in range(TB):
                    mm = nc.tensor.transpose(bank4[:, t, :], xn[:, t, :], ident[:, :])
            elif name in "qk":
                pe.wait_ge(s_taken["hT"], beta + 1)
                mm = nc.tensor.matmul(bank, (wq if name == "q" else wk)[:, :], hT[:, :], start=True, stop=True)
            elif name == "v":
                for t in range(TB):
                    mm = nc.tensor.matmul(bank4[:, t, :], hT[:, t * P:(t + 1) * P], wv[:, :], start=True, stop=True)
            elif name == "x1":
                pe.wait_ge(s_att, beta + 1)
                pe.wait_ge(s_wog, beta + 1)
                for t in range(TB):
                    mm = nc.tensor.matmul(bank4[:, t, :], num[:, t * P:(t + 1) * P], woG[:, :], start=True, stop=True)
            elif name == "h2T":
                pe.wait_ge(s_x1n, beta + 1)
                for t in range(TB):
                    mm = nc.tensor.transpose(bank4[:, t, :], x1n[:, t, :], ident[:, :])
            elif name[:2] == "l0":
                pe.wait_ge(s_taken["h2T"], beta + 1)
                if isinstance(beta, int) and beta == 0:
                    pe.wait_ge(s_wts, 2)
                    pe.wait_ge(s_W0, 2)
                m = int(name[3])
                mm = nc.tensor.matmul(bank, W0[:, m * P:(m + 1) * P], h2T[:, :], start=True, stop=True)
            elif name[:2] == "l1":
                if first:
                    for m in range(KC):
                        pe.wait_ge(s_taken[f"l0_{m}"], beta + 1)
                m = int(name[3])
                for kc in chunks:
                    mm = nc.tensor.matmul(bank, W1[:, kc, m * P:(m + 1) * P], hid[0][:, kc, :],
                                          start=(kc == 0), stop=(kc == KC - 1))
            elif name == "y":
                if first:
                    pe.wait_ge(s_w2g, beta + 1)
                    for m in range(KC):
                        pe.wait_ge(s_taken[f"l1_{m}"], beta + 1)
                for t in chunks:
                    for kc in range(KC):
                        mm = nc.tensor.matmul(bank4[:, t, :], hid[1][:, kc, t * P:(t + 1) * P], W2G[:, kc, :],
                                              start=(kc == 0), stop=(kc == KC - 1))
            if last:
                mm.then_inc(s_made[name], 1)

        def pe_batch(pe, b):
            def scores(b, n, h):
                if n == H:
                    b, n = b + 1, 0
                if not live(b):
                    return
                if n % QUAD == 0 and h == 0:
                    need(pe, s_mrow[n // QUAD], (b + 1) * PARTS * 16)
                if isinstance(b, int) and b == 0 and n == 0:
                    pe.wait_ge(s_mx, 2 * QUAD * TB - 4 + 2 * h)
                if n:
                    z_taken(pe, b, n - 1, h)
                elif not isinstance(b, int) or b:
                    z_taken(pe, b - 1, H - 1, h)
                for t in range(2):
                    k0_ = (2 * h + t) * P
                    mm = nc.tensor.matmul(Z[:, h, t * S:(t + 1) * S], KH[:, n, k0_:k0_ + P], QH[:, n, :],
                                          start=True, stop=True)
                mm.then_inc(s_z, 1)

            def logits(n, qts):
                beta, g = (b, n // QUAD + 2) if n < 8 else (b + 1, n // QUAD - 2)
                if not live(beta):
                    return
                hh = QUAD * g + n % QUAD
                if n == 8 and qts[0] == 0 and is_first(b):
                    pe.wait_ge(s_gate, 1)
                if n % QUAD == 0 and qts[0] == 0:
                    need(pe, s_qk[g], (beta + 1) * E_DMAS * 16)
                for qt in qts:
                    i = 64 * beta + TB * hh + qt
                    if is_first(b):
                        need(pe, s_mx, i // 2 * 2 - 4)
                    else:
                        need(pe, s_mx, i - 1)
                    if n % QUAD == 0 and qt == TB - 1:
                        need(pe, s_ms, NQ * beta + g)
                    nc.tensor.matmul(logits_bank(b, beta, hh, qt)[:, qt % 2, :], QH[0:MROW, hh, qt * P:(qt + 1) * P], KH[0:MROW, hh, :],
                                     start=True, stop=True).then_inc(s_a, 1)

            def maxima_across(n):
                beta, g = quad_before(b, n)
                if n % QUAD or not live(beta):
                    return
                follows = n != 8 or live(b + 1)
                pe.wait_ge(s_mx, TB * H * beta + TB * QUAD * (g + 1) + (2 if follows else 0))
                nc.tensor.transpose(SA[0:QUAD * TB, 1, 0:P], mx[:, g % 2, :], ident[:, :]).then_inc(s_mt, 1)

            def with_v(n):
                q = (n - LAG) // QUAD - 1
                tb = (n - LAG) % QUAD
                beta, g = (b, q) if q >= 0 else (b - 1, q + NQ)
                if not live(beta):
                    return
                if tb == 0:
                    need(pe, s_p, H * beta + QUAD * g + QUAD)
                    need(pe, s_vq, NQ * beta + g + 1)
                    need(pe, s_ot, NQ * beta + g)
                for j in range(QUAD):
                    hh = QUAD * g + j
                    mm = nc.tensor.matmul(OP[32 * j:32 * j + 2 * HD, :], Vq[:, tb, hh, :, :].rearrange("p d a -> p (d a)"),
                                          prob[:, hh % P_RING, tb * S:(tb + 1) * S],
                                          start=(tb == 0), stop=(tb == TB - 1), skip_group_check=True)
                mm.then_inc(s_pv, 1)

            for n in range(H):
                logits(n, (0, 1))
                with_v(n)
                scores(b, n + 1, 0)
                misc_at(pe, b, n, 0)
                logits(n, (2,))
                maxima_across(n)
                logits(n, (3,))
                misc_at(pe, b, n, 1)
                scores(b, n + 1, 1)

        def misc_at(pe, b, n, place):
            for i, (_, _, pieces, _) in enumerate(misc_of(b)):
                done = 0
                for step, where, count in pieces:
                    if (step, where) == (n, place):
                        misc_product(pe, b, i, range(done, done + count))
                    done += count

        @block.tensor
        def _(pe):
            pe_setup(pe)
            batches(lambda b: pe_batch(pe, b))(nc.tensor)

        def act_setup(act):
            nc.scalar.preload_act_table_set("natural_log_exp_and_others")
            act.wait_ge(ld_c, 16)
            nc.scalar.activation(c_exp, c_rows, ACT.Exp, scale=-1.0).then_inc(s_cexp, 1)
            act.wait_ge(s_eps, 1)
            act.wait_ge(s_mv1, 1)
            nc.scalar.activation(rs1[:, :], mv1[:, :, 1], ACT.Ln, bias=epst[:, 0:1]).then_inc(s_ln1, 1)
            act.wait_ge(s_ln1, 1)
            nc.scalar.activation(rs1[:, :], rs1[:, :], ACT.Exp, scale=-0.5).then_inc(s_rs1, 1)
            act.wait_ge(s_mod, 3)

        def act_batch(act, b):
            def from_z(n, h):
                if not live(b):
                    return
                i = 2 * H * b + 2 * n + h
                need(act, s_z, i + 1)
                if h == 0 and PATHS[n] == "A":
                    k = before("AV", n) - 1
                    need(act, s_cp, b * N_P + k - 1)
                    nc.scalar.activation(zc[:, k % 2, :], Z[:, h, 0:S], ACT.Copy).then_inc(s_za, 1)
                part = of_vector(n, h)
                need(act, s_cv, i - 1)
                nc.scalar.activation(sq[:, h, part], Z[:, h, part], ACT.Square).then_inc(s_sq, 1)

            def log_of(n):
                beta, m = (b, n - 1) if n else (b - 1, H - 1)
                if live(beta):
                    cubic_ready(act, beta, m, 0)
                    cubic_ready(act, beta, m, 1)
                    nc.scalar.activation(cub[:, m % F_RING], cub[:, m % F_RING], ACT.Ln, scale=-1.0,
                                         bias=2.0).then_inc(s_ln, 1)

            def exp_of(n):
                beta, m = (b, n - 1) if n else (b - 1, H - 1)
                if live(beta):
                    need(act, s_ln, H * beta + m + 1)
                    if isinstance(beta, int) and beta == 0 and m == 0:
                        act.wait_ge(s_wts, 2)
                        act.wait_ge(s_W0, 2)
                        act.wait_ge(s_gw, 16)
                    need(act, s_pv, QUAD * (NQ * beta + m // QUAD - 1))
                    nc.scalar.activation(prob[:, m % P_RING, :], cub[:, m % F_RING].rearrange("p a n -> p (a n)"),
                                         ACT.Exp, scale=-1.0).then_inc(s_p, 1)

            def misc(n, place):
                def at(step, where, beta):
                    return (n, place) == (step, where) and live(beta)

                for name, beta, bank in products_at(b, n, "sme") if place else ():
                    if name == "hT":
                        act.wait_ge(s_made["hT"], beta + 1)
                        need(act, s_made["v"], beta)
                        nc.scalar.activation(hT[:, :], bank, ACT.Identity, scale=col(1, beta), bias=col(0, beta))\
                            .then_inc(s_taken["hT"], 1)
                    if name in "qk" and is_first(b):
                        act.wait_ge(s_made[name], beta + 1)
                        nc.scalar.activation((SQ if name == "q" else SK)[:, 0, :], bank, ACT.Copy,
                                             scale=SCALE if name == "q" else 1.0).then_inc(s_part1, 1)
                    if name == "h2T":
                        act.wait_ge(s_made["h2T"], beta + 1)
                        need(act, s_made["l0_3"], beta)
                        nc.scalar.activation(h2T[:, :], bank, ACT.Identity, scale=col(3, beta), bias=col(2, beta))\
                            .then_inc(s_taken["h2T"], 1)
                if at(*event(b, "den_ln"), b - 1):
                    for g in range(2):
                        act.wait_ge(s_gat[g], b * (NQ // 2) * QUAD * 16)
                    nc.scalar.activation(den, den, ACT.Ln).then_inc(s_dln, 1)
                if at(*event(b, "den_exp"), b - 1):
                    act.wait_ge(s_dln, b)
                    nc.scalar.activation(den, den, ACT.Exp, scale=-1.0).then_inc(s_dinv, 1)
                if at(9, 0, b + 2):
                    act.wait_ge(s_mv1, b + 3)
                    need(act, s_xn, b + 2)
                    nc.scalar.activation(rs1[:, :], mv1[:, :, 1], ACT.Ln, bias=epst[:, 0:1]).then_inc(s_ln1, 1)
                if at(9, 1, b + 2):
                    act.wait_ge(s_ln1, b + 3)
                    nc.scalar.activation(rs1[:, :], rs1[:, :], ACT.Exp, scale=-0.5).then_inc(s_rs1, 1)
                if at(*event(b, "rs2_ln"), b - 1):
                    act.wait_ge(s_mv2, b)
                    need(act, s_x1n, b - 1)
                    nc.scalar.activation(rs2[:, :], mv2[:, :, 1], ACT.Ln, bias=epst[:, 0:1]).then_inc(s_ln2, 1)
                if at(*event(b, "rs2_exp"), b - 1):
                    act.wait_ge(s_ln2, b)
                    nc.scalar.activation(rs2[:, :], rs2[:, :], ACT.Exp, scale=-0.5).then_inc(s_rs2, 1)

            for n in range(H):
                from_z(n, 0)
                log_of(n)
                misc(n, 0)
                from_z(n, 1)
                exp_of(n)
                misc(n, 1)

        @block.scalar
        def _(act):
            act_setup(act)
            batches(lambda b: act_batch(act, b))(nc.scalar)

        def dve_setup(dve):
            nc.vector.memset(epst[:, :], EPS).then_inc(s_eps, 1)
            dve.wait_ge(s_xa, 16)
            for t in range(TB):
                bn = nc.vector.bn_stats(st1[:, t, :], xa[:, t, :])
            bn.then_inc(s_st1, 1)
            dve.wait_ge(s_st1, 1)
            for t in range(TB):
                bn = nc.vector.bn_aggr(mv1[:, t, :], st1[:, t, :])
            bn.then_inc(s_mv1, 1)
            dve.wait_ge(s_cexp, 1)
            nc.vector.tensor_scalar(c_exp, c_exp, 1.0, None, ALU.add).then_inc(s_silu, 1)
            dve.wait_ge(s_silu, 1)
            nc.vector.reciprocal(c_inv, c_exp).then_inc(s_silu, 1)
            dve.wait_ge(s_silu, 2)
            nc.vector.tensor_tensor(c_sil, c_rows, c_inv, ALU.mult).then_inc(s_silu, 1)
            dve.wait_ge(s_rs1, 1)
            for t in range(TB):
                last = nc.vector.tensor_scalar(xn[:, t, :], xa[:, t, :], mv1[:, t, 0:1], rs1[:, t:t + 1],
                                               ALU.subtract, ALU.mult)
            last.then_inc(s_xn, 1)
            dve.wait_ge(s_csT, 1)
            nc.vector.tensor_copy(csil, MB[:, 0:B]).then_inc(s_csil, 1)
            dve.wait_ge(s_wT, 1)
            for i, w in enumerate((wq, wk)):
                nc.vector.tensor_copy(w[:, :].rearrange("p (g d j) -> p g d j", g=NQ, d=HD),
                                      SA[:, 0, i * D:(i + 1) * D].rearrange("p (g j d) -> p g d j", g=NQ, d=HD))
            nc.vector.tensor_copy(wv[:, :], SA[:, 0, 2 * D:3 * D])
            nc.vector.tensor_copy(wo[:, :], SA[:, 0, 3 * D:4 * D]).then_inc(s_wcp, 1)
            dve.wait_ge(s_modp, 1)
            M4 = MB[:, 64:64 + 4 * B].rearrange("p (i b) -> p i b", i=4)
            nc.vector.tensor_copy(mod[:, :, :], M4).then_inc(s_mod, 1)
            dve.wait_ge(s_mod, 1)
            for i in (1, 3):
                nc.vector.tensor_scalar(mod[:, i, :], mod[:, i, :], 1.0, None, ALU.add).then_inc(s_mod, 1)

        def dve_gates(dve):
            dve.wait_ge(s_gatep, 1)
            nc.vector.tensor_copy(g_in, SA[0:B, 1, 0:2 * D]).then_inc(s_gate, 1)
            dve.wait_ge(s_gate, 1)
            nc.vector.tensor_scalar(g_sign, g_in, 0.0, 2.0, ALU.is_ge, ALU.mult)
            nc.vector.tensor_scalar(g_abs, g_in, -1.0, None, ALU.mult).then_inc(s_gate, 1)
            dve.wait_ge(s_gate, 2)
            nc.vector.tensor_tensor(g_abs, g_abs, g_in, ALU.max).then_inc(s_gate, 1)
            dve.wait_ge(s_gate, 3)
            nc.vector.tensor_scalar(g_abs, g_abs, 0.25, None, ALU.max)
            nc.vector.tensor_scalar(g_sign, g_sign, -1.0, None, ALU.add).then_inc(s_gate, 1)
            dve.wait_ge(s_gate, 4)
            nc.vector.tensor_tensor(g_sign, g_sign, g_abs, ALU.mult).then_inc(s_gate, 1)
            dve.wait_ge(s_gate, 5)
            dve.wait_ge(ld_s, 4 * 16)
            nc.vector.tensor_scalar(g_row[:, 0:D], g_sign[:, 0:D], 1.0, None, ALU.mult)
            nc.vector.tensor_tensor(g_row[:, D:2 * D], g_sign[:, 0:D], bo8, ALU.mult)
            nc.vector.tensor_scalar(g_row[:, 2 * D:3 * D], g_sign[:, D:2 * D], sv[0:B, 2:3], None, ALU.mult)\
                .then_inc(s_gate, 1)
            nc.vector.tensor_scalar(sv[:, 0:2], sv[:, 0:2], 2.0, None, ALU.mult).then_inc(s_sv, 1)
            nc.vector.memset(OP[:, :], 0.0)
            dve.wait_ge(s_sv, 1)
            dve.wait_ge(ld_k, 3 * 16)
            nc.vector.tensor_tensor(W0[:, :], k0u[:, 0, :], k0u[:, 1, :], ALU.subtract).then_inc(s_W0, 1)
            dve.wait_ge(s_W0, 1)
            nc.vector.tensor_scalar(W0[:, :], W0[:, :], 2.0, None, ALU.mult).then_inc(s_W0, 1)

        def dve_batch(dve, b):
            def from_z(n, h):
                if not live(b):
                    return
                if h == 0 and PATHS[n] == "V":
                    k = before("AV", n) - 1
                    need(dve, s_z, 2 * H * b + 2 * n + 1)
                    need(dve, s_cp, b * N_P + k - 1)
                    nc.vector.tensor_copy(zc[:, k % 2, :], Z[:, h, 0:S]).then_inc(s_zv, 1)
                need(dve, s_sq, 2 * H * b + 2 * n + h + 1)
                need(dve, s_p, H * b + n + 1 - F_RING)
                part = of_vector(n, h)
                nc.vector.scalar_tensor_tensor(cub[:, n % F_RING, h, part], sq[:, h, part], 3.0, Z[:, h, part],
                                               ALU.add, ALU.mult).then_inc(s_cv, 1)

            def maxima(n, qts):
                beta, g = (b, n // QUAD + 2) if n < 8 else (b + 1, n // QUAD - 2)
                if not live(beta):
                    return
                j = n % QUAD
                i = TB * H * beta + TB * (QUAD * g + j) + qts[0]
                need(dve, s_a, i + len(qts))
                if j == 0 and qts[0] == 0:
                    need(dve, s_mt, NQ * beta + g - 1)
                nc.vector.tensor_reduce(mx[:, g % 2, j * TB + qts[0]:j * TB + qts[-1] + 1],
                                        logits_bank(b, beta, QUAD * g + j, qts[0])[:, qts[0] % 2:qts[-1] % 2 + 1, :],
                                        AX_X, ALU.max).then_inc(s_mx, len(qts))

            def take_maxima(n):
                beta, g = quad_before(b, n)
                if n % QUAD or not live(beta):
                    return
                i = NQ * beta + g
                dve.wait_ge(s_mt, i + 1)
                need(dve, s_mp, 4 * i)
                nc.vector.tensor_scalar(ms[:, :], SA[0:QUAD * TB, 1, 0:P], -1.0, -1.0, ALU.mult, ALU.add)\
                    .then_inc(s_ms, 1)

            def relu_of(name, beta, bank):
                layer, m = int(name[1]), int(name[3])
                dve.wait_ge(s_made[name], beta + 1)
                last = "l1_3" if layer == 0 else "y"
                if m == 0:
                    need(dve, s_made[last], beta)
                nc.vector.tensor_scalar(hid[layer][:, m, :], bank, sv[:, layer:layer + 1], 0.0, ALU.mult, ALU.max)\
                    .then_inc(s_taken[name], 1)

            def misc(n, place):
                def at(step, where, beta):
                    return (n, place) == (step, where) and live(beta)

                if n % QUAD == (LAG + QUAD - 1) % QUAD and place == 1:
                    q = (n - LAG) // QUAD - 1
                    beta, g = (b, q) if q >= 0 else (b - 1, q + NQ)
                    if live(beta):
                        i = NQ * beta + g
                        dve.wait_ge(s_pv, QUAD * (i + 1))
                        need(dve, s_gat[g % 2], (2 * beta + g // 2) * QUAD * 16)
                        nc.vector.tensor_copy(OT[:, g % 2, :], OP[:, :]).then_inc(s_ot, 1)
                if at(6, 0, b + 2):
                    dve.wait_ge(s_xa, 16 * (b + 3))
                    for t in range(TB):
                        bn = nc.vector.bn_stats(st1[:, t, :], xa[:, t, :])
                    bn.then_inc(s_st1, 1)
                if at(7, 1, b + 2):
                    dve.wait_ge(s_st1, b + 3)
                    need(dve, s_xn, b + 2)
                    apart(dve, b)
                    for t in range(TB):
                        bn = nc.vector.bn_aggr(mv1[:, t, :], st1[:, t, :])
                    bn.then_inc(s_mv1, 1)
                if at(*event(b, "st2"), b - 1):
                    dve.wait_ge(s_taken["x1"], b)
                    for t in range(TB):
                        bn = nc.vector.bn_stats(st2[:, t, :], x1[:, t, :])
                    bn.then_inc(s_st2, 1)
                if at(*event(b, "mv2"), b - 1):
                    dve.wait_ge(s_st2, b)
                    need(dve, s_x1n, b - 1)
                    apart(dve, b)
                    for t in range(TB):
                        bn = nc.vector.bn_aggr(mv2[:, t, :], st2[:, t, :])
                    bn.then_inc(s_mv2, 1)
                if at(*event(b, "att")[:2], b - 1) and event(b, "att")[2] == "dve":
                    dve.wait_ge(s_dinv, b)
                    nc.vector.tensor_tensor(num, num, den, ALU.mult).then_inc(s_att, 1)
                if at(*event(b, "x1n")[:2], b - 1) and event(b, "x1n")[2] == "dve":
                    dve.wait_ge(s_rs2, b)
                    need(dve, s_made["h2T"], b - 1)
                    for t in range(TB):
                        last = nc.vector.tensor_scalar(x1n[:, t, :], x1[:, t, :], mv2[:, t, 0:1], rs2[:, t:t + 1],
                                                       ALU.subtract, ALU.mult)
                    last.then_inc(s_x1n, 1)

            def take_products(b, n, point):
                for name, beta, bank in products_at(b, n, point):
                    bank4 = bank.rearrange("p (t d) -> p t d", t=TB)
                    if name in "qk":
                        i = "qk".index(name)
                        need(dve, s_part3, 2 * (beta - 1) + i + 1)
                        if is_first(b):
                            dve.wait_ge(s_part1, i + 1)
                            nc.vector.scalar_tensor_tensor(rem[:, i, :], bank, (SCALE, 1.0)[i], (SQ, SK)[i][:, 0, :],
                                                           ALU.mult, ALU.subtract).then_inc(s_taken[name], 1)
                        else:
                            dve.wait_ge(s_made[name], beta + 1)
                            nc.vector.tensor_scalar(rem[:, i, :], bank, (SCALE, 1.0)[i], None, ALU.mult)\
                                .then_inc(s_taken[name], 1)
                    elif name[0] == "l":
                        relu_of(name, beta, bank)
                    elif name == "x1":
                        dve.wait_ge(s_made["x1"], beta + 1)
                        dve.wait_ge(s_xbg, beta + 1)
                        need(dve, s_x1k, beta)
                        need(dve, s_x1n, beta)
                        nc.vector.tensor_tensor(x1[:, :, :], bank4, xb[:, :, :], ALU.add).then_inc(s_taken["x1"], 1)
                    elif name == "v":
                        dve.wait_ge(s_made["v"], beta + 1)
                        need(dve, s_vq, NQ * beta)
                        nc.vector.tensor_copy(Vn[:, :, :, :].rearrange("p t h d -> p t (h d)"), bank4)\
                            .then_inc(s_taken["v"], 1)
                    elif name == "y":
                        dve.wait_ge(s_made["y"], beta + 1)
                        need(dve, s_x1k, beta + 1)
                        need(dve, s_out, 16 * beta)
                        nc.vector.tensor_tensor(y[:, :, :], bank4, x1k[:, :, :], ALU.add).then_inc(s_taken["y"], 1)

            for n in range(H):
                from_z(n, 0)
                if n == 0 and isinstance(b, int) and b == B:
                    take_products(b - 1, H, "s")
                take_products(b, n, "s")
                maxima(n, (0, 1))
                take_products(b, n, "m")
                misc(n, 0)
                from_z(n, 1)
                take_maxima(n)
                if n % QUAD:
                    maxima(n, (2, 3))
                else:
                    maxima(n, (2,))
                    maxima(n, (3,))
                take_products(b, n, "e")
                misc(n, 1)
                if n == 5 and is_first(b):
                    dve_gates(dve)

        @block.vector
        def _(dve):
            dve_setup(dve)
            batches(lambda b: dve_batch(dve, b))(nc.vector)

        def pool_setup(pool):
            nc.gpsimd.memset(ident[:, :], 0.0).then_inc(s_id, 1)
            pool.wait_ge(s_id, 1)
            nc.gpsimd.affine_select(out=ident[:, :], in_=ident[:, :], compare_op=ALU.not_equal, fill=1.0, base=0,
                                    pattern=[[-1, P]], channel_multiplier=1).then_inc(s_id, 1)
            for t in (QH, KH):
                nc.gpsimd.memset(t[:, :, :].bitcast(F32), 0.0).then_inc(s_one, 1)
            pool.wait_ge(s_one, 2)
            nc.gpsimd.memset(KH[MROW:MROW + PARTS, :, :].bitcast(F32), TWO_ONES).then_inc(s_one, 1)
            pool.wait_ge(s_one, 3)
            nc.gpsimd.memset(Vq[:, :, :, :, :], 1.0).then_inc(s_one, 1)
            pool.wait_ge(ld_k, 3 * 16)
            nc.gpsimd.tensor_scalar(W1[:, :, :], k1u, 2.0, -1.0, ALU.mult, ALU.add).then_inc(s_wts, 1)
            nc.gpsimd.tensor_scalar(W2[:, :, :], k2u, 2.0, -1.0, ALU.mult, ALU.add).then_inc(s_wts, 1)

        def pool_batch(pool, b):
            def from_z(n):
                if not live(b) or PATHS[n] == "D":
                    return
                k = before("AV", n) - 1
                if PATHS[n] == "A":
                    need(pool, s_za, b * N_A + before("A", n))
                else:
                    need(pool, s_zv, b * N_V + before("V", n))
                need(pool, s_p, H * b + n + 1 - F_RING)
                zz, cc = zc[:, k % 2, :], cub[:, n % F_RING, 0, 0:S]
                nc.gpsimd.tensor_tensor(cc, zz, zz, ALU.mult).then_inc(s_q1, 1)
                need(pool, s_q1, 2 * (b * N_P + k) + 1)
                apart(pool, b)
                nc.gpsimd.tensor_scalar(cc, cc, 1.0, 3.0, ALU.mult, ALU.add).then_inc(s_q1, 1)
                need(pool, s_q1, 2 * (b * N_P + k) + 2)
                nc.gpsimd.tensor_tensor(cc, cc, zz, ALU.mult).then_inc(s_cp, 1)

            def normalise(beta, src, mv, rs, dst, s_rs, s_free, s_done, free):
                pool.wait_ge(s_rs, beta + 1)
                need(pool, s_free, free)
                apart(pool, beta)
                for t in range(TB):
                    last = nc.gpsimd.tensor_scalar(dst[:, t, :], src[:, t, :], mv[:, t, 0:1], rs[:, t:t + 1],
                                                   ALU.subtract, ALU.mult)
                last.then_inc(s_done, 1)

            def v_in(beta, g):
                if live(beta):
                    i = NQ * beta + g
                    pool.wait_ge(s_taken["v"], beta + 1)
                    need(pool, s_pv, QUAD * (i + 1 - NQ))
                    apart(pool, beta)
                    hs = slice(QUAD * g, QUAD * (g + 1))
                    nc.gpsimd.tensor_copy(Vq[:, :, hs, :, 0], Vn[:, :, hs, :]).then_inc(s_vq, 1)

            def misc(n, place):
                def at(step, where, beta):
                    return (n, place) == (step, where) and live(beta)

                for i, (step, dst) in enumerate(((2, SQ), (3, SK))):
                    if at(step, 0, b + 1):
                        k = 2 * (b + 1) + i + 1
                        pool.wait_ge(s_taken["qk"[i]], b + 2)
                        if not is_first(b):
                            need(pool, s_parts["qk"[i]], (b + 1) * PARTS * 16)
                            apart(pool, b)
                            nc.gpsimd.tensor_scalar(dst[:, 0, :], rem[:, i, :], 1.0, 0.0, ALU.mult, ALU.add)\
                                .then_inc(s_part1, 1)
                            pool.wait_ge(s_part1, k)
                            nc.gpsimd.tensor_tensor(rem[:, i, :], rem[:, i, :], dst[:, 0, :], ALU.subtract)\
                                .then_inc(s_rem, 1)
                            pool.wait_ge(s_rem, k - 2)
                            apart(pool, b)
                        nc.gpsimd.tensor_scalar(dst[:, 1, :], rem[:, i, :], 1.0, 0.0, ALU.mult, ALU.add)\
                            .then_inc(s_part2, 1)
                        pool.wait_ge(s_part2, k)
                        nc.gpsimd.tensor_tensor(dst[:, 2, :], rem[:, i, :], dst[:, 1, :], ALU.subtract)\
                            .then_inc(s_part3, 1)
                if n % QUAD == 1 and place == 0:
                    beta, gg = quad_before(b, n - 1)
                    if live(beta):
                        k = 4 * (NQ * beta + gg)
                        pool.wait_ge(s_ms, NQ * beta + gg + 1)
                        need(pool, s_mrow[(gg - 1) % NQ], (beta + (gg > 0)) * PARTS * 16)
                        apart(pool, b)
                        nc.gpsimd.tensor_scalar(mp[:, 0, :], ms[:, :], 1.0, 0.0, ALU.mult, ALU.add).then_inc(s_mp, 1)
                        pool.wait_ge(s_mp, k + 1)
                        nc.gpsimd.tensor_tensor(mrem[:, :], ms[:, :], mp[:, 0, :], ALU.subtract)\
                            .then_inc(s_mp, 1)
                        pool.wait_ge(s_mp, k + 2)
                        apart(pool, b)
                        nc.gpsimd.tensor_scalar(mp[:, 1, :], mrem[:, :], 1.0, 0.0, ALU.mult, ALU.add).then_inc(s_mp, 1)
                        pool.wait_ge(s_mp, k + 3)
                        nc.gpsimd.tensor_tensor(mp[:, 2, :], mrem[:, :], mp[:, 1, :], ALU.subtract)\
                            .then_inc(s_mp, 1)
                if at(*event(b, "att")[:2], b - 1) and event(b, "att")[2] == "pool":
                    pool.wait_ge(s_dinv, b)
                    nc.gpsimd.tensor_tensor(num, num, den, ALU.mult)\
                        .then_inc(s_att, 1)
                if at(*event(b, "w2g"), b - 2):
                    pool.wait_ge(s_gB, 16 * (b - 1))
                    need(pool, s_made["y"], b - 2)
                    for kc in range(KC):
                        tt = nc.gpsimd.tensor_tensor(W2G[:, kc, :], W2[:, kc, :], gB[:, :], ALU.mult)
                    tt.then_inc(s_w2g, 1)
                if at(*event(b, "wog"), b - 1):
                    pool.wait_ge(s_gA, 16 * b)
                    need(pool, s_made["x1"], b - 1)
                    nc.gpsimd.tensor_tensor(woG[:, :], wo[:, :], gA[:, 0:D], ALU.mult).then_inc(s_wog, 1)
                if at(*event(b, "xbg"), b - 1):
                    pool.wait_ge(s_xb, 16 * b)
                    for t in range(TB):
                        tt = nc.gpsimd.tensor_tensor(xb[:, t, :], xb[:, t, :], gA[:, D:2 * D], ALU.add)
                    tt.then_inc(s_xbg, 1)
                if at(10, 1, b + 2):
                    normalise(b + 2, xa, mv1, rs1, xn, s_rs1, s_made["hT"], s_xn, b + 2)
                if at(0, 0, b - 2) :
                    pool.wait_ge(s_taken["x1"], b - 1)
                    need(pool, s_taken["y"], b - 2)
                    apart(pool, b)
                    nc.gpsimd.tensor_scalar(x1k[:, :, :], x1[:, :, :], 1.0, 0.0, ALU.mult, ALU.add).then_inc(s_x1k, 1)
                if at(*event(b, "x1n")[:2], b - 1) and event(b, "x1n")[2] == "pool":
                    normalise(b - 1, x1, mv2, rs2, x1n, s_rs2, s_made["h2T"], s_x1n, b - 1)
                if (n, place) == (3, 1):
                    v_in(b, 2)
                if (n, place) == (6, 0):
                    v_in(b, 3)
                if (n, place) == (15, 1):
                    v_in(b + 1, 0)
                    v_in(b + 1, 1)

            for n in range(H):
                from_z(n)
                misc(n, 0)
                misc(n, 1)

        @block.gpsimd
        def _(pool):
            pool_setup(pool)
            batches(lambda b: pool_batch(pool, b))(nc.gpsimd)

        def sp_setup(sp):
            sp.dma_start(xa[:, :, :], x_t[:, 0:TB, :]).then_inc(s_xa, 16)
            sp.dma_start(c_rows, c).then_inc(ld_c, 16)
            sp.dma_start(w_rows[:, 0:3, :], w_qkv.rearrange("(k p) d -> p k d", p=P)).then_inc(ld_w, 16)
            sp.dma_start(wm, wmod).then_inc(ld_w, 16)
            sp.dma_start(w_rows[:, 3, :], w_out).then_inc(ld_w, 16)
            for i, s in enumerate((s0, s1, s2)):
                sp.dma_start(sv[:, i:i + 1], s.partition_broadcast(P)).then_inc(ld_s, 16)
            sp.dma_start(bo8, b_out.partition_broadcast(B)).then_inc(ld_s, 16)
            sp.dma_start(k0u, k0.rearrange("(a p) n -> p a n", p=P)).then_inc(ld_k, 16)
            sp.dma_start(k1u, k1.rearrange("(a p) n -> p a n", p=P)).then_inc(ld_k, 16)
            sp.dma_start(k2u, k2.rearrange("(a p) n -> p a n", p=P)).then_inc(ld_k, 16)

        def sp_need(sp, b, s, n):
            need(sp, s, n)
            apart(sp, b)

        def sp_batch(sp, b):
            for g in range(NQ):
                if g == 0 and live(b - 1):
                    if isinstance(b, int) and b == 1:
                        sp.wait_ge(s_gw, 16)
                    sp_need(sp, b, s_xbg, b - 1)
                    sp.dma_start(gA[:, :], gate_rows[bass.ds(b - 1, 1), 0:2 * D].partition_broadcast(P)).then_inc(s_gA, 16)
                if g == 0 and live(b - 2):
                    sp_need(sp, b, s_w2g, b - 2)
                    sp.dma_start(gB[:, :], gate_rows[bass.ds(b - 2, 1), 2 * D:3 * D].partition_broadcast(P)).then_inc(s_gB, 16)
                if g == 1 and live(b + 1):
                    sp_need(sp, b, s_qk[NQ - 1], (b + 1) * E_DMAS * 16)
                    for i, (src, dst) in enumerate(((SQ, parts_q), (SK, parts_k))):
                        for a in range(PARTS):
                            if a < 2:
                                sp_need(sp, b, s_part3 if a else s_part1, 2 * (b + 1) + i + 1)
                            sp.dma_start(dst[:, a], src[:, a, :]).then_inc(s_parts["qk"[i]], 16)
                beta, gg = (b, NQ - 1) if g == 0 else (b + 1, g - 1)
                if live(beta):
                    sp_need(sp, b, s_z, 2 * QUAD * (NQ * (beta - 1) + gg + 1))
                    if isinstance(beta, int) and beta == 0 and gg == 0:
                        sp.wait_ge(s_one, 3)
                    heads = slice(QUAD * gg, QUAD * gg + QUAD)
                    if g == 1:
                        sp_need(sp, b, s_parts["q"], (beta + 1) * PARTS * 16)
                    for a in range(PARTS):
                        r = a * PARTS * HD
                        rows = parts_q[gg, a].rearrange("(d j) s -> d (j s)", d=HD)
                        sp.dma_start(QH[r:r + PARTS * HD, heads, :], rows.partition_broadcast(PARTS)).then_inc(s_qk[gg], 16)
                    if g == 1:
                        sp_need(sp, b, s_parts["k"], (beta + 1) * PARTS * 16)
                    rows = parts_k[gg].rearrange("c (d j) s -> (c d) (j s)", d=HD)
                    sp.dma_start(KH[0:NROW, heads, :], rows.partition_broadcast(PARTS)).then_inc(s_qk[gg], 16)
                if g == 2 and is_first(b):
                    sp.wait_ge(s_gate, 6)
                    sp.dma_start(gate_rows, g_row).then_inc(s_gw, 16)
                if g == 0 and live(b + 2):
                    sp_need(sp, b, s_xn, b + 2)
                    sp.dma_start(xa[:, :, :], x_t[:, bass.ds((b + 2) * TB, TB), :]).then_inc(s_xa, 16)
                if g == 0 and live(b - 1):
                    sp_need(sp, b, s_taken["x1"], b - 1)
                    sp.dma_start(xb[:, :, :], x_t[:, bass.ds((b - 1) * TB, TB), :]).then_inc(s_xb, 16)
                beta, gg = (b, g + 1) if g < NQ - 1 else (b + 1, 0)
                if live(beta):
                    sp_need(sp, b, s_mp, 4 * (NQ * beta + gg + 1))
                    for a in range(PARTS):
                        sp.dma_start(QH[MROW + a:MROW + a + 1, QUAD * gg:QUAD * gg + QUAD, :], mp[:, a, :])\
                            .then_inc(s_mrow[gg], 16)
                beta, gg = (b, g - 2) if g >= 2 else (b - 1, g + 2)
                if live(beta):
                    sp_need(sp, b, s_ot, NQ * beta + gg + 1)
                    if gg == 0:
                        sp_need(sp, b, s_made["x1"], beta)
                    for j in range(QUAD):
                        r = 32 * gg + HD * j
                        sp.dma_start(nd[r:r + HD, :, :], OT[32 * j:32 * j + 2 * HD, gg % 2, :]).then_inc(s_gat[gg % 2], 16)
                if g == 3 and live(b - 2):
                    sp_need(sp, b, s_taken["y"], b - 1)
                    sp.dma_start(out_t[:, bass.ds((b - 2) * TB, TB), :], y[:, :, :]).then_inc(s_out, 16)

        @block.sync
        def _(sp):
            sp_setup(sp)
            batches(lambda b: sp_batch(sp, b))(nc.sync)
            sp.wait_ge(s_out, 16 * B)


_INS = ["L0_attn_x", "L0_attn_w_qkv", "L0_attn_w_out", "L0_attn_b_out", "L0_ffn_k0", "L0_ffn_k1", "L0_ffn_k2",
        "L0_ffn_s0", "L0_ffn_s1", "L0_ffn_s2", "L0_c", "L0_wmod"]


def kernel(**inputs):
    import numpy as np
    import concourse.bacc as bacc
    from concourse.bass_utils import run_bass_kernel_spmd

    nc = bacc.Bacc("TRN2", target_bir_lowering=False, num_devices=1)
    arrays, args = {}, []
    for name in _INS:
        a = np.ascontiguousarray(inputs[name])
        if a.ndim == 0:
            a = a.reshape(1)
        arrays[name] = a
        args.append(nc.dram_tensor(name, a.shape, mybir.dt.from_np(a.dtype), kind="ExternalInput").ap())
    out = nc.dram_tensor("out", (B, S, D), F32, kind="ExternalOutput").ap()
    adaln_block(nc, *args, out)
    r = run_bass_kernel_spmd(nc, [arrays], core_ids=[0])
    return r.results[0]["out"]
```
